# Optimizing a Trainium2 kernel written in Bass

```python
import numpy as np
import jax
import jax.numpy as jnp

def _softmax(x, axis=-1):
    return jax.nn.softmax(x, axis=axis)

def _gelu(x):
    return jax.nn.gelu(x, approximate=True)

def _silu(x):
    return jax.nn.silu(x)

def _sigmoid(x):
    return jax.nn.sigmoid(x)

def _layernorm(x, axis=-1, eps=1e-05):
    m = jnp.mean(x, axis=axis, keepdims=True)
    v = jnp.var(x, axis=axis, keepdims=True)
    return (x - m) / jnp.sqrt(v + eps)

def _scatter_add(tgt, idx, src, axis=0):
    return tgt.at[idx].add(src)

def _segment_sum(src, seg, n):
    return jax.ops.segment_sum(src, seg, n)
kernel_name = 'mk_seq_postln_d1_jaxref_r8_343fdb'

def setup_inputs(seed: int=0):
    np.random.seed(seed)
    _w = jnp.asarray

    def _L0_attn_setup():
        import jax, jax.numpy as jnp
        import numpy as np
        NUM_HEADS = 16
        HIDDEN = 128
        HEAD_DIM = HIDDEN // NUM_HEADS
        B, L = (2, 256)
        key = jax.random.key(seed)
        ks = jax.random.split(key, 5)
        scale = 1.0 / np.sqrt(HIDDEN)
        return {'x': jax.random.normal(ks[0], (B, L, HIDDEN), dtype=jnp.float32), 'Wq': jax.random.normal(ks[1], (HIDDEN, HIDDEN), dtype=jnp.float32) * scale, 'Wk': jax.random.normal(ks[2], (HIDDEN, HIDDEN), dtype=jnp.float32) * scale, 'Wv': jax.random.normal(ks[3], (HIDDEN, HIDDEN), dtype=jnp.float32) * scale, 'Wo': jax.random.normal(ks[4], (HIDDEN, HIDDEN), dtype=jnp.float32) * scale}
    _L0_attn_in = _L0_attn_setup()

    def _L0_ffn_setup():
        import jax, jax.numpy as jnp
        import numpy as np
        B, L, D = (2, 128, 128)
        HID, E, K = (256, 8, 2)
        key = jax.random.key(seed)
        ks = jax.random.split(key, 4)
        std = 0.02
        return {'x': jax.random.normal(ks[0], (B, L, D), dtype=jnp.float32), 'router_scale': jnp.ones((D,), dtype=jnp.float32), 'router_w': jax.random.normal(ks[1], (D, E), dtype=jnp.float32) * std, 'gating_w': jax.random.normal(ks[2], (E, 2, HID, D), dtype=jnp.float32) * std, 'linear_w': jax.random.normal(ks[3], (E, HID, D), dtype=jnp.float32) * std, 'per_expert_scale': jnp.ones((E,), dtype=jnp.float32)}
    _L0_ffn_in = _L0_ffn_setup()
    _d = {'L0_attn_x': _L0_attn_in['x'], 'L0_attn_Wq': _L0_attn_in['Wq'], 'L0_attn_Wk': _L0_attn_in['Wk'], 'L0_attn_Wv': _L0_attn_in['Wv'], 'L0_attn_Wo': _L0_attn_in['Wo'], 'L0_ffn_router_scale': _L0_ffn_in['router_scale'], 'L0_ffn_router_w': _L0_ffn_in['router_w'], 'L0_ffn_gating_w': _L0_ffn_in['gating_w'], 'L0_ffn_linear_w': _L0_ffn_in['linear_w'], 'L0_ffn_per_expert_scale': _L0_ffn_in['per_expert_scale']}
    _x0 = _d['L0_attn_x']
    _d['L0_attn_x'] = jax.random.normal(jax.random.fold_in(jax.random.key(seed), 1), (1, 2048, 128), dtype=_x0.dtype)
    del _x0
    return _d

def reference(L0_attn_x, L0_attn_Wq, L0_attn_Wk, L0_attn_Wv, L0_attn_Wo, L0_ffn_router_scale, L0_ffn_router_w, L0_ffn_gating_w, L0_ffn_linear_w, L0_ffn_per_expert_scale):

    def _L0_attn_ref(x, Wq, Wk, Wv, Wo):
        import jax, jax.numpy as jnp
        import numpy as np
        NUM_HEADS = 16
        HIDDEN = 128
        HEAD_DIM = HIDDEN // NUM_HEADS
        B, L = (2, 256)
        b, l, _ = x.shape
        q = (x @ Wq.T).reshape(b, l, NUM_HEADS, HEAD_DIM)
        k = (x @ Wk.T).reshape(b, l, NUM_HEADS, HEAD_DIM)
        v = (x @ Wv.T).reshape(b, l, NUM_HEADS, HEAD_DIM)
        q = jax.nn.elu(q) + 1.0
        k = jax.nn.elu(k) + 1.0
        kv = jnp.einsum('blhd,blhe->blhde', k, v)
        kv_cumsum = jnp.cumsum(kv, axis=1)
        k_cumsum = jnp.cumsum(k, axis=1)
        out = jnp.einsum('blhd,blhde->blhe', q, kv_cumsum)
        normalizer = jnp.clip(jnp.einsum('blhd,blhd->blh', q, k_cumsum), 1e-06, None)
        out = out / normalizer[..., None]
        out = out.reshape(b, l, HIDDEN)
        return out @ Wo.T

    def _L0_ffn_ref(x, router_scale, router_w, gating_w, linear_w, per_expert_scale):
        import jax, jax.numpy as jnp
        import numpy as np
        B, L, D = (2, 128, 128)
        HID, E, K = (256, 8, 2)
        d = x.shape[-1]
        var = jnp.mean(jnp.square(x), axis=-1, keepdims=True)
        r_in = x * jax.lax.rsqrt(var + 1e-06)
        r_in = r_in * jax.lax.rsqrt(jnp.array(d, dtype=r_in.dtype)) * router_scale
        logits = jnp.dot(r_in, router_w).astype(jnp.float32)
        probs = jax.nn.softmax(logits, axis=-1)
        _, top_k_idx = jax.lax.top_k(logits, K)
        indicator = jax.nn.one_hot(top_k_idx, probs.shape[-1], dtype=probs.dtype)
        gate_weights = indicator.sum(axis=-2) * probs
        renorm = jnp.sum(gate_weights, axis=-1, keepdims=True)
        renorm = jnp.where(renorm > 0.0, renorm, 1.0)
        weights = probs / renorm
        top_k_w = jnp.take_along_axis(weights, top_k_idx, axis=-1)
        combine = jnp.einsum('blke,blk->ble', indicator, top_k_w)
        combine = combine * per_expert_scale
        gate0 = jnp.einsum('bld,ehd->bleh', x, gating_w[:, 0])
        gate1 = jnp.einsum('bld,ehd->bleh', x, gating_w[:, 1])
        act = jax.nn.gelu(gate0) * gate1
        out = jnp.einsum('bleh,ehd,ble->bld', act, linear_w, combine)
        return out.astype(x.dtype)
    x = L0_attn_x
    x = _layernorm(x + _L0_attn_ref(x, L0_attn_Wq, L0_attn_Wk, L0_attn_Wv, L0_attn_Wo), axis=-1)
    x = _layernorm(x + _L0_ffn_ref(x, L0_ffn_router_scale, L0_ffn_router_w, L0_ffn_gating_w, L0_ffn_linear_w, L0_ffn_per_expert_scale), axis=-1)
    return x

_drawn_inputs = setup_inputs


def setup_inputs(seed=0):
    import zlib

    import numpy as np

    out = dict(_drawn_inputs(seed))
    spreads = {'L0_ffn_router_scale': (1.0, 0.6), 'L0_ffn_per_expert_scale': (1.0, 0.6)}
    factors = {'L0_attn_Wq': 3.459,
     'L0_ffn_router_w': 8.0,
     'L0_ffn_gating_w': 8.0,
     'L0_ffn_linear_w': 8.0}
    for name, (base, spread) in spreads.items():
        noise = np.random.default_rng([zlib.crc32(name.encode()), seed]).standard_normal(out[name].shape)
        drawn = base * np.exp(spread * noise) if base else spread * noise
        out[name] = jnp.asarray(drawn.astype(out[name].dtype))
    for name, factor in factors.items():
        out[name] = (out[name] * factor).astype(out[name].dtype)
    return out
```

```python
from contextlib import ExitStack

import concourse.bass as bass
from concourse import mybir
from concourse.alu_op_type import AluOpType as ALU

F32 = mybir.dt.float32
I32 = mybir.dt.int32
U32 = mybir.dt.uint32
ACT = mybir.ActivationFunctionType
AX = mybir.AxisListType

P = 128
D = 128
T = 2048
CHUNKS = T // P
GROUP = 4
GROUPS = CHUNKS // GROUP
H, HD = 16, 8
HE = HD + 1
KV = H * HE * HD
HEADS = [(0, 6), (6, 12), (12, 16)]
E, K, HID = 8, 2, 256
HB = HID // P
REGION = T + P
SPARE = E * REGION
TILES = T * K // P + E - 1
PADS = E + E - 1
ROW = D + 2 * E
BUFS = 3
assert TILES % BUFS == 0
LN_EPS, RMS_EPS, DEN_MIN = 1e-5, 1e-6, 1e-6
BELOW = -3.0e38

CONST = {}
_at = 0
for _name, _n in (("tri", P), ("stri", P), ("ident", P), ("ones", P), ("block", H * HE), ("desc", GROUP * E),
                  ("tok", GROUP), ("ebase", E), ("tile", TILES), ("half", GROUP), ("pad", PADS)):
    CONST[_name] = (_at, _at + _n)
    _at += _n
NCONST = _at



class Steps:

    def __init__(self, eng, sem):
        self.eng, self.sem, self.base, self.n = eng, sem, 0, 0

    def start(self, base):
        self.base, self.n = base, 0

    def did(self, ins):
        ins.then_inc(self.sem, 1)
        self.n += 1
        return self.base + self.n

    def need(self, mark):
        self.eng.wait_ge(self.sem, mark)

    def chain(self, ins):
        self.need(self.did(ins))


def build(nc, xT, x, wqkv, wo, rw, rscale, pes, gate_w, lin_w, consts, out):
    zbuf = nc.dram_tensor("zbuf", (SPARE + (E - 1) * P, ROW), F32, kind="Internal").ap()
    planes = nc.dram_tensor("planes", (K * T + PADS * P, D), F32, kind="Internal").ap()

    with ExitStack() as ctx:
        def sb(name, shape, dt=F32):
            return ctx.enter_context(nc.sbuf_tensor(name, shape, dt))

        def bank(name, shape):
            return ctx.enter_context(nc.psum_tensor(name, shape, F32))

        def sem(name):
            return ctx.enter_context(nc.semaphore(name))

        C = sb("C", [P, NCONST])

        def const(name):
            a, b = CONST[name]
            return C[:, a:b]

        w_qkv = sb("w_qkv", [P, 3 * D])
        w_o = sb("w_o", [P, D])
        w_r0 = sb("w_r0", [P, E])
        w_rs = sb("w_rs", [P, 1])
        w_r = sb("w_r", [P, E])
        pes_b = sb("pes_b", [P, E])
        w_g = sb("w_g", [P, E * 2 * HID])
        w_l = sb("w_l", [P, E * HB * D])
        xTs = sb("xTs", [P, GROUP, P])
        xs = sb("xs", [P, GROUP, D])
        eqk = sb("eqk", [P, 2, 2 * D])
        rqk = sb("rqk", [P, 2, 2 * D])
        qk = sb("qk", [P, 2, 2 * D])
        v1 = sb("v1", [P, 2, H * HE])
        kv = sb("kv", [P, 2, KV])
        prod = sb("prod", [P, KV])
        num = sb("num", [P, H * HE])
        num2 = sb("num2", [P, H * HE])
        den = sb("den", [P, H])
        rden = sb("rden", [P, H])
        o = sb("o", [P, 2, D])
        qT = sb("qT", [P, 2, P])
        oT = sb("oT", [P, 2, P])
        state_m = sb("state_m", [P, 2, H * HE])
        pads = sb("pads", [P, PADS, ROW])
        zero = sb("zero", [P, H * HE])
        y = sb("y", [P, GROUP, D])
        junk = sb("junk", [P, 2, D])
        rows = sb("rows", [P, GROUP, ROW])
        zT = sb("zT", [P, GROUP, P])
        lgs = sb("lgs", [P, GROUP, E])
        ysum = sb("ysum", [P, GROUP])
        negm = sb("negm", [P, GROUP])
        ssq = sb("ssq", [P, GROUP])
        vare = sb("vare", [P, GROUP])
        rstd = sb("rstd", [P, GROUP])
        shift = sb("shift", [P, GROUP])
        zsq = sb("zsq", [P, GROUP])
        zsqe = sb("zsqe", [P, GROUP])
        rrms = sb("rrms", [P, GROUP])
        names = ["logit", "eq1", "key1", "ind1", "rest", "eq2", "key2", "ind2", "dlog", "elog", "prob", "ind", "gw",
                 "comb", "pos"]
        R = {n: sb("r_" + n, [P, GROUP, E]) for n in names}
        names1 = ["m1", "k1", "m2", "k2", "esum", "einv", "ren", "reng", "renr"]
        R1 = {n: sb("r_" + n, [P, GROUP]) for n in names1}
        tok = sb("tok", [P, GROUP])
        base = sb("base", [P, GROUP + 1, E])
        pos12 = sb("pos12", [P, K * GROUP, E])
        slot_f = sb("slot_f", [P, K * GROUP])
        slot = sb("slot", [P, K * GROUP], I32)
        cnt_i = sb("cnt_i", [P, E], I32)
        nt_f = sb("nt_f", [P, E])
        nt_i = sb("nt_i", [P, E], I32)
        nt_s = sb("nt_s", [P, E], I32)
        ntile = sb("ntile", [P, E])
        cumA = sb("cumA", [P, E])
        cumB = sb("cumB", [P, E])
        cumC = sb("cumC", [P, E])
        skip = sb("skip", [P, E])
        past = sb("past", [1, TILES, E])
        pskip = sb("pskip", [1, TILES, E])
        te_f = sb("te_f", [1, TILES])
        tr_f = sb("tr_f", [1, TILES])
        tr_g = sb("tr_g", [1, TILES])
        tile_e = sb("tile_e", [1, TILES], I32)
        tile_r = sb("tile_r", [1, TILES], I32)
        zin = sb("zin", [P, BUFS, ROW])
        zinT = sb("zinT", [P, BUFS, P])
        wcol = sb("wcol", [P, BUFS])
        dst = sb("dst", [P, BUFS], I32)
        gelu = sb("gelu", [P, BUFS, HID])
        act = sb("act", [P, BUFS, HID])
        actT = sb("actT", [P, BUFS, HB, P])
        yout = sb("yout", [P, BUFS, D])
        zall = sb("zall", [P, CHUNKS, D])
        pl = sb("pl", [P, K, CHUNKS, D])
        s1 = sb("s1", [P, CHUNKS, D])
        s2 = sb("s2", [P, CHUNKS, D])
        fsum = sb("fsum", [P, CHUNKS])
        fneg = sb("fneg", [P, CHUNKS])
        fssq = sb("fssq", [P, CHUNKS])
        fvar = sb("fvar", [P, CHUNKS])
        frs = sb("frs", [P, CHUNKS])
        fshift = sb("fshift", [P, CHUNKS])
        res = sb("res", [P, CHUNKS, D])

        B = [bank(f"bank{i}", [P, 512]) for i in range(8)]
        qkv_ps = B[0]
        pre_ps = B[2:5]
        state_ps = B[5][:, 0:H * HE]
        turn_ps = B[1]
        qT_ps, oT_ps, lg_ps = B[1][:, 0:P], B[1][:, 0:P], B[1][:, 0:GROUP * E]
        rank_ps, tot_ps = B[1][:, 0:GROUP * E], B[1][:, GROUP * E:2 * GROUP * E]
        inter_ps = B[6][:, 0:H * HE]
        y_ps = B[7][:, 0:D]
        gate_ps = B[0:3]
        zinT_ps = B[3][:, 0:P]
        actT_ps = B[4:7]
        yout_ps = B[7][:, 0:D]

        w_loaded = sem("w_loaded")
        c_loaded = sem("c_loaded")
        wr_loaded = sem("wr_loaded")
        we_loaded = sem("we_loaded")
        xT_loaded = [sem(f"xT_loaded{j}") for j in range(GROUP)]
        x_loaded = [sem(f"x_loaded{j}") for j in range(GROUP)]
        set_up = sem("set_up")
        pool_set_up = sem("pool_set_up")
        state_zero = sem("state_zero")
        qkv_done = sem("qkv_done")
        act_in = sem("act_in")
        phi_done = sem("phi_done")
        kv_done = sem("kv_done")
        qTp_done = sem("qTp_done")
        qT_done = sem("qT_done")
        pre_done = sem("pre_done")
        pre_used = sem("pre_used")
        state_used = sem("state_used")
        inter_done = sem("inter_done")
        state_done = sem("state_done")
        inter_used = sem("inter_used")
        o_done = sem("o_done")
        oTp_done = sem("oTp_done")
        oT_done = sem("oT_done")
        y_done = sem("y_done")
        r1_done = sem("r1_done")
        negm_done = sem("negm_done")
        ssq_done = sem("ssq_done")
        vare_done = sem("vare_done")
        rstd_done = sem("rstd_done")
        shift_done = sem("shift_done")
        z_done = sem("z_done")
        zsq_done = sem("zsq_done")
        zTp_done = sem("zTp_done")
        zT_done = sem("zT_done")
        lg_done = sem("lg_done")
        lgs_done = sem("lgs_done")
        zsqe_done = sem("zsqe_done")
        rrms_done = sem("rrms_done")
        dlog_done = sem("dlog_done")
        elog_done = sem("elog_done")
        ind_done = sem("ind_done")
        rank_done = sem("rank_done")
        route_done = sem("route_done")
        scattered = sem("scattered")
        z_saved = sem("z_saved")
        cnt_done = sem("cnt_done")
        table_done = sem("table_done")
        padded = sem("padded")
        zin_loaded = [sem(f"zin_loaded{j}") for j in range(BUFS)]
        zinTp_done = sem("zinTp_done")
        zinT_done = sem("zinT_done")
        meta_done = sem("meta_done")
        gate_done = sem("gate_done")
        gelu_done = sem("gelu_done")
        act_done = sem("act_done")
        actTp_done = sem("actTp_done")
        actT_done = sem("actT_done")
        yp_done = sem("yp_done")
        yout_done = sem("yout_done")
        placed = [sem(f"placed{j}") for j in range(BUFS)]
        pl_loaded = [sem(f"pl_loaded{g}") for g in range(GROUPS)]
        fsum_done = sem("fsum_done")
        fneg_done = sem("fneg_done")
        fssq_done = sem("fssq_done")
        fvar_done = sem("fvar_done")
        frs_done = sem("frs_done")
        fshift_done = sem("fshift_done")
        res_done = sem("res_done")
        stored = sem("stored")
        pads_done = sem("pads_done")
        scatter_go = sem("scatter_go")
        dve_steps = sem("dve_steps")
        act_steps = sem("act_steps")

        def groups(eng, body):
            body(0, True)
            with eng.Fori(1, GROUPS) as g:
                body(g, False)

        block = ctx.enter_context(nc.Block())

        @block.sync
        def _(sp):
            sp.dma_start(w_qkv[:, :], wqkv).then_inc(w_loaded, 16)
            for j in range(GROUP):
                sp.dma_start(xTs[:, j, :], xT[:, j * P:(j + 1) * P]).then_inc(xT_loaded[j], 16)
                if j == 0:
                    sp.dma_start(C[:, :], consts).then_inc(c_loaded, 16)
                sp.dma_start(xs[:, j, :], x[j * P:(j + 1) * P, :]).then_inc(x_loaded[j], 16)
            sp.dma_start(w_o[:, :], wo).then_inc(wr_loaded, 16)
            sp.dma_start(w_rs[:, :], rscale).then_inc(z_saved, 16)
            sp.dma_start(pes_b[:, :], pes).then_inc(wr_loaded, 16)
            sp.dma_start(w_g[:, :], gate_w).then_inc(we_loaded, 16)
            sp.dma_start(w_l[:, :], lin_w).then_inc(we_loaded, 16)

            def save_z(g):
                sp.wait_ge(z_done, GROUP * g + GROUP)
                sp.dma_start(zall[:, bass.ds(GROUP * g, GROUP), :], rows[:, :, 0:D]).then_inc(z_saved, 16)

            with sp.Fori(1, GROUPS) as g:
                for j in range(GROUP):
                    n = GROUP * g + j
                    sp.wait_ge(qkv_done, n - GROUP + 1)
                    sp.dma_start(xTs[:, j, :], xT[:, bass.ds(n * P, P)]).then_inc(xT_loaded[j], 16)
                for j in range(GROUP):
                    n = GROUP * g + j
                    sp.wait_ge(r1_done, n - GROUP + 1)
                    sp.dma_start(xs[:, j, :], x[bass.ds(n * P, P), :]).then_inc(x_loaded[j], 16)
                save_z(g - 1)
            save_z(GROUPS - 1)

            sp.wait_ge(cnt_done, 1)
            sp.wait_ge(pads_done, 1)
            end = sp.alloc_register("rows_end")
            for e in range(E):
                sp.reg_load(end, cnt_i[0:1, e:e + 1])
                at = sp.snap(end, min_val=0, max_val=SPARE - P)
                sp.dma_start(zbuf[bass.ds(at, P), :], pads[:, e, :]).then_inc(padded, 16)
            sp.dma_start(zbuf[SPARE:, :].rearrange("(b p) r -> p b r", p=P), pads[:, E:, :]).then_inc(padded, 16)
            sp.wait_ge(table_done, 1)
            sp.wait_ge(padded, 16 * (E + 1))
            sp.wait_ge(scattered, 16 * (K * CHUNKS + 1))
            row = sp.alloc_register("tile_row")
            for b in range(BUFS):
                sp.reg_load(row, tile_r[0:1, b:b + 1])
                at = sp.snap(row, min_val=0, max_val=SPARE + (E - 2) * P)
                sp.dma_start(zin[:, b, :], zbuf[bass.ds(at, P), :]).then_inc(zin_loaded[b], 16)
            with sp.Fori(1, TILES // BUFS) as i:
                for b in range(BUFS):
                    k = BUFS * i + b
                    sp.reg_load(row, tile_r[0:1, bass.ds(k, 1)])
                    at = sp.snap(row, min_val=0, max_val=SPARE + (E - 2) * P)
                    sp.wait_ge(meta_done, 2 * (k - BUFS + 1))
                    sp.dma_start(zin[:, b, :], zbuf[bass.ds(at, P), :]).then_inc(zin_loaded[b], 16)
            for b in range(BUFS):
                sp.wait_ge(placed[b], 16 * (TILES // BUFS))
            for g in range(GROUPS):
                for k in range(K):
                    at = k * T + g * GROUP * P
                    sp.dma_start(pl[:, k, g * GROUP:(g + 1) * GROUP, :],
                                 planes[at:at + GROUP * P, :].rearrange("(c p) d -> p c d", p=P))\
                      .then_inc(pl_loaded[g], 16)
            for g in range(GROUPS):
                sp.wait_ge(res_done, GROUP * (g + 1))
                sp.dma_start(out[g * GROUP * P:(g + 1) * GROUP * P, :].rearrange("(c p) d -> p c d", p=P),
                             res[:, g * GROUP:(g + 1) * GROUP, :]).then_inc(stored, 16)
            sp.wait_ge(stored, 16 * GROUPS)

        @block.gpsimd
        def _(pool):
            pool.dma_start(w_r0[:, :], rw).then_inc(scattered, 16)
            pool.memset(v1[:, :, :], 1.0).then_inc(pool_set_up, 1)
            pool.memset(pads[:, :, :], 0.0).then_inc(pool_set_up, 1)
            pool.wait_ge(c_loaded, 16)
            pool.wait_ge(pool_set_up, 2)
            pool.tensor_copy(pads[:, :, D + E:], const("pad").unsqueeze(2).to_broadcast([P, PADS, E]))\
                .then_inc(pads_done, 1)

            def outer(g, j):
                n, s = GROUP * g + j, j % 2
                pool.wait_ge(phi_done, n + 1)
                pool.wait_ge(act_in, 3 * (n + 1))
                if not (isinstance(g, int) and n < 2):
                    pool.wait_ge(pre_done, 3 * (n - 1))
                a = v1[:, s, :].rearrange("p (h e) -> p h e", e=HE).unsqueeze(3).to_broadcast([P, H, HE, HD])
                b = qk[:, s, D:2 * D].rearrange("p (h d) -> p h d", d=HD).unsqueeze(2).to_broadcast([P, H, HE, HD])
                pool.tensor_tensor(kv[:, s, :].rearrange("p (h e d) -> p h e d", e=HE, d=HD), a, b,
                                   ALU.mult).then_inc(kv_done, 1)

            def norm_pow(g):
                pool.wait_ge(vare_done, g + 1)
                pool.tensor_tensor(rstd[:, :], vare[:, :], const("half"), ALU.pow).then_inc(rstd_done, 1)

            def rms_pow(g):
                pool.wait_ge(zsqe_done, g + 1)
                pool.tensor_tensor(rrms[:, :], zsqe[:, :], const("half"), ALU.pow).then_inc(rrms_done, 1)

            def scatter(g):
                pool.wait_ge(route_done, g + 1)
                pool.wait_ge(z_done, GROUP * g + GROUP)
                pool.sem_inc(scatter_go, 1)
                for j in range(GROUP):
                    for c in (j, GROUP + j):
                        pool.indirect_dma_start(
                            zbuf, bass.IndirectOffsetOnAxis(ap=slot[:, c:c + 1].bitcast(U32), axis=0),
                            rows[:, j, :], None).then_inc(scattered, 16)

            def body(g, first):
                for j in range(GROUP):
                    outer(g, j)
                    if not first and j == 2:
                        norm_pow(g - 1)
                    if not first and j == 3:
                        rms_pow(g - 1)
                        scatter(g - 1)

            groups(pool, body)
            norm_pow(GROUPS - 1)
            rms_pow(GROUPS - 1)
            scatter(GROUPS - 1)

            def place(k, b):
                pool.wait_ge(yout_done, k + 1)
                pool.wait_ge(meta_done, 2 * (k + 1))
                pool.sem_inc(scatter_go, 1)
                pool.indirect_dma_start(
                    planes, bass.IndirectOffsetOnAxis(ap=dst[:, b:b + 1].bitcast(U32), axis=0),
                    yout[:, b, :], None).then_inc(placed[b], 16)

            with pool.Fori(0, TILES // BUFS) as i:
                for b in range(BUFS):
                    place(BUFS * i + b, b)
            for g in range(GROUPS):
                c = slice(GROUP * g, GROUP * g + GROUP)
                pool.wait_ge(fvar_done, g + 1)
                pool.tensor_tensor(frs[:, c], fvar[:, c], const("half"), ALU.pow).then_inc(frs_done, 1)

        @block.tensor
        def _(pe):
            def project(g, j):
                n, s = GROUP * g + j, j % 2
                pe.wait_ge(xT_loaded[j], 16 * (g + 1))
                if not (isinstance(g, int) and n < 1):
                    pe.wait_ge(act_in, 3 * n)
                pe.matmul(qkv_ps[:, 0:3 * D], xTs[:, j, :], w_qkv[:, :], start=True, stop=True)\
                  .then_inc(qkv_done, 1)

            def attend(g, j, before=""):
                n, s = GROUP * g + j, j % 2
                start = isinstance(g, int) and n < 1
                pe.wait_ge(phi_done, n + 1)
                if not (isinstance(g, int) and n < 2):
                    pe.wait_ge(oT_done, n - 1)
                if before == "logits":
                    pe.wait_ge(lgs_done, g)
                if before == "ranks":
                    pe.wait_ge(phi_done, n + 2)
                pe.transpose(qT_ps, qk[:, s, 0:D], const("ident")).then_inc(qTp_done, 1)
                pe.wait_ge(kv_done, n + 1)
                for b, (h0, h1) in enumerate(HEADS):
                    if not start:
                        pe.wait_ge(pre_used, 3 * (n - 1) + b + 1)
                    c0, c1 = h0 * HE * HD, h1 * HE * HD
                    pe.matmul(pre_ps[b][:, 0:c1 - c0], const("tri"), kv[:, s, c0:c1], start=True, stop=True)\
                      .then_inc(pre_done, 1)
                pe.wait_ge(qT_done, n + 1)
                pe.wait_ge(state_used, n + 1)
                if not start:
                    pe.wait_ge(inter_used, n)
                pe.matmul(inter_ps, qT[:, s, :], state_m[:, s, :], start=True, stop=True).then_inc(inter_done, 1)
                pe.matmul(state_ps, qk[:, s, D:2 * D], v1[:, s, :], start=False, stop=False,
                          skip_group_check=True).then_inc(state_done, 1)

            def finish(g, j, last=None):
                n, s = GROUP * g + j, j % 2
                start = isinstance(g, int) and n < 1
                pe.wait_ge(o_done, n + 1)
                pe.wait_ge(qT_done, n + 2 if last is None else last)
                pe.transpose(oT_ps, o[:, s, :], const("ident")).then_inc(oTp_done, 1)
                pe.wait_ge(oT_done, n + 1)
                if not start:
                    pe.wait_ge(r1_done, n)
                pe.matmul(y_ps, oT[:, s, :], w_o[:, :], start=True, stop=True).then_inc(y_done, 1)

            def logits(g):
                pe.wait_ge(z_done, GROUP * g + GROUP)
                for i in range(GROUP):
                    t = pe.transpose(turn_ps[:, i * P:(i + 1) * P], rows[:, i, 0:D], const("ident"))
                t.then_inc(zTp_done, 1)
                pe.wait_ge(zT_done, g + 1)
                for i in range(GROUP):
                    t = pe.matmul(lg_ps[:, E * i:E * i + E], zT[:, i, :], w_r[:, :], start=True, stop=True)
                t.then_inc(lg_done, 1)

            def ranks(g):
                pe.wait_ge(ind_done, g + 1)
                pe.wait_ge(lgs_done, g + 1)
                flat = R["ind"][:, :, :].rearrange("p c e -> p (c e)")
                pe.matmul(rank_ps, const("stri"), flat, start=True, stop=True).then_inc(rank_done, 1)
                pe.matmul(tot_ps, const("ones"), flat, start=True, stop=True).then_inc(rank_done, 1)

            pe.wait_ge(c_loaded, 16)
            pe.wait_ge(set_up, 3)
            pe.wait_ge(pool_set_up, 2)
            pe.matmul(state_ps, zero[:, 0:P], zero[:, :], start=True, stop=False, skip_group_check=True)\
              .then_inc(state_zero, 1)
            pe.wait_ge(w_loaded, 16)
            pe.wait_ge(wr_loaded, 32)

            def body(g, first):
                for j in range(GROUP):
                    project(g, j)
                    if j >= 1:
                        attend(g, j - 1, "logits" if j == 3 and not first else "")
                    elif not first:
                        attend(g - 1, GROUP - 1, "ranks")
                    if j >= 2:
                        finish(g, j - 2)
                    elif not first:
                        finish(g - 1, GROUP - 2 + j)
                    if not first and j == 2:
                        logits(g - 1)
                    if not first and j == 3:
                        ranks(g - 1)

            groups(pe, body)
            pe.wait_ge(route_done, GROUPS - 1)
            attend(GROUPS - 1, GROUP - 1)
            finish(GROUPS - 1, GROUP - 2, CHUNKS)
            pe.wait_ge(oT_done, CHUNKS - 1)
            finish(GROUPS - 1, GROUP - 1, CHUNKS)
            logits(GROUPS - 1)
            ranks(GROUPS - 1)

            def turn_in(k, b, rnd):
                pe.wait_ge(zin_loaded[b], 16 * (rnd + 1))
                if not (isinstance(k, int) and k < 1):
                    pe.wait_ge(zinT_done, k)
                pe.transpose(zinT_ps, zin[:, b, 0:D], const("ident")).then_inc(zinTp_done, 1)

            expert = pe.alloc_register("expert")

            def gates(k, b):
                pe.reg_load(expert, tile_e[0:1, bass.ds(k, 1)] if not isinstance(k, int) else tile_e[0:1, k:k + 1])
                ex = pe.snap(expert, min_val=0, max_val=E - 1)
                pe.wait_ge(zinT_done, k + 1)
                pe.matmul(gate_ps[b][:, :], zinT[:, b, :], w_g[:, bass.ds(ex * (2 * HID), 2 * HID)],
                          start=True, stop=True).then_inc(gate_done, 1)

            def output(k, b):
                pe.wait_ge(act_done, k + 1)
                for h in range(HB):
                    mm = pe.transpose(actT_ps[b][:, h * P:(h + 1) * P], act[:, b, h * P:(h + 1) * P], const("ident"))
                mm.then_inc(actTp_done, 1)
                pe.reg_load(expert, tile_e[0:1, bass.ds(k, 1)] if not isinstance(k, int) else tile_e[0:1, k:k + 1])
                ex = pe.snap(expert, min_val=0, max_val=E - 1)
                pe.wait_ge(actT_done, k + 1)
                if not (isinstance(k, int) and k < 1):
                    pe.wait_ge(yout_done, k)
                for h in range(HB):
                    mm = pe.matmul(yout_ps, actT[:, b, h, :], w_l[:, bass.ds(ex * (HB * D) + h * D, D)],
                                   start=(h == 0), stop=(h == HB - 1))
                mm.then_inc(yp_done, 1)

            pe.wait_ge(we_loaded, 32)
            pe.wait_ge(table_done, 1)
            pe.wait_ge(route_done, GROUPS)
            pe.wait_ge(r1_done, CHUNKS)
            turn_in(0, 0, 0)
            turn_in(1, 1, 0)
            gates(0, 0)
            turn_in(2, 2, 0)
            gates(1, 1)
            output(0, 0)
            with pe.Fori(1, TILES // BUFS) as i:
                for b in range(BUFS):
                    k = BUFS * i + b
                    turn_in(k, b, i)
                    gates(k - 1, (b - 1) % BUFS)
                    output(k - 2, (b - 2) % BUFS)
            gates(TILES - 1, (TILES - 1) % BUFS)
            output(TILES - 2, (TILES - 2) % BUFS)
            output(TILES - 1, (TILES - 1) % BUFS)

        @block.scalar
        def _(ac):
            st = Steps(ac, act_steps)

            def inputs(g, j):
                n, s = GROUP * g + j, j % 2
                ac.wait_ge(qkv_done, n + 1)
                if not (isinstance(g, int) and n < 2):
                    ac.wait_ge(phi_done, n - 1)
                    ac.wait_ge(state_done, n - 1)
                    ac.wait_ge(kv_done, n - 1)
                ac.activation(eqk[:, s, :], qkv_ps[:, 0:2 * D], ACT.Exp).then_inc(act_in, 1)
                ac.activation(rqk[:, s, :], qkv_ps[:, 0:2 * D], ACT.Relu).then_inc(act_in, 1)
                ac.activation(v1[:, s, :].rearrange("p (h e) -> p h e", e=HE)[:, :, 0:HD],
                              qkv_ps[:, 2 * D:3 * D].rearrange("p (h d) -> p h d", d=HD),
                              ACT.Copy).then_inc(act_in, 1)

            def copy_qT(g, j):
                n, s = GROUP * g + j, j % 2
                ac.wait_ge(qTp_done, n + 1)
                if not (isinstance(g, int) and n < 2):
                    ac.wait_ge(inter_done, n - 1)
                ac.copy(qT[:, s, :], qT_ps).then_inc(qT_done, 1)

            def copy_oT(g, j):
                n, s = GROUP * g + j, j % 2
                ac.wait_ge(oTp_done, n + 1)
                if not (isinstance(g, int) and n < 2):
                    ac.wait_ge(y_done, n - 1)
                ac.copy(oT[:, s, :], oT_ps).then_inc(oT_done, 1)

            def spread(g):
                ac.wait_ge(negm_done, g + 1)
                for i in range(GROUP):
                    if i:
                        ac.wait_ge(ssq_done, GROUP * g + i)
                    ac.activation(junk[:, 0, :], y[:, i, :], ACT.Square, bias=negm[:, i:i + 1],
                                  accum_out=ssq[:, i:i + 1]).then_inc(ssq_done, 1)

            def normalise(g):
                ac.wait_ge(shift_done, g + 1)
                ac.wait_ge(rstd_done, g + 1)
                ac.wait_ge(scattered, 16 * (K * GROUP * g + 1))
                ac.wait_ge(z_saved, 16 * (g + 1))
                for i in range(GROUP):
                    ac.activation(rows[:, i, 0:D], y[:, i, :], ACT.Identity, bias=shift[:, i:i + 1],
                                  scale=rstd[:, i:i + 1]).then_inc(z_done, 1)
                for i in range(GROUP):
                    ac.wait_ge(z_done, GROUP * g + i + 1)
                    if i:
                        ac.wait_ge(zsq_done, GROUP * g + i)
                    ac.activation(junk[:, 1, :], rows[:, i, 0:D], ACT.Square,
                                  accum_out=zsq[:, i:i + 1]).then_inc(zsq_done, 1)

            def copy_zT(g):
                ac.wait_ge(zTp_done, g + 1)
                ac.copy(zT[:, :, :].rearrange("p c t -> p (c t)"), turn_ps[:, :]).then_inc(zT_done, 1)
                ac.wait_ge(lg_done, g + 1)
                ac.copy(lgs[:, :, :].rearrange("p c e -> p (c e)"), lg_ps).then_inc(lgs_done, 1)

            def exp_logits(g):
                ac.wait_ge(dlog_done, g + 1)
                ac.activation(R["elog"][:, :, :], R["dlog"][:, :, :], ACT.Exp).then_inc(elog_done, 1)

            ac.wait_ge(pool_set_up, 2)

            def body(g, first):
                for j in range(GROUP):
                    inputs(g, j)
                    if j >= 1:
                        copy_qT(g, j - 1)
                    elif not first:
                        copy_qT(g - 1, GROUP - 1)
                    if j >= 2:
                        copy_oT(g, j - 2)
                    elif not first:
                        copy_oT(g - 1, GROUP - 2 + j)
                    if not first and j == 1:
                        spread(g - 1)
                    if not first and j == 2:
                        normalise(g - 1)
                        copy_zT(g - 1)
                    if not first and j == 3:
                        exp_logits(g - 1)

            groups(ac, body)
            copy_qT(GROUPS - 1, GROUP - 1)
            copy_oT(GROUPS - 1, GROUP - 2)
            copy_oT(GROUPS - 1, GROUP - 1)
            spread(GROUPS - 1)
            normalise(GROUPS - 1)
            copy_zT(GROUPS - 1)
            exp_logits(GROUPS - 1)

            def copy_zinT(k, b):
                ac.wait_ge(zinTp_done, k + 1)
                if not (isinstance(k, int) and k < BUFS):
                    ac.wait_ge(gate_done, k - BUFS + 1)
                ac.copy(zinT[:, b, :], zinT_ps).then_inc(zinT_done, 1)

            def gelu_gate(k, b):
                ac.wait_ge(gate_done, k + 1)
                if not (isinstance(k, int) and k < BUFS):
                    ac.wait_ge(act_done, k - BUFS + 1)
                ac.activation(gelu[:, b, :], gate_ps[b][:, 0:HID], ACT.Gelu_apprx_tanh).then_inc(gelu_done, 1)

            def copy_actT(k, b):
                ac.wait_ge(actTp_done, k + 1)
                ac.copy(actT[:, b, :, :].rearrange("p h t -> p (h t)"), actT_ps[b][:, 0:HID]).then_inc(actT_done, 1)

            copy_zinT(0, 0)
            copy_zinT(1, 1)
            gelu_gate(0, 0)
            copy_zinT(2, 2)
            gelu_gate(1, 1)
            copy_actT(0, 0)
            with ac.Fori(1, TILES // BUFS) as i:
                for b in range(BUFS):
                    k = BUFS * i + b
                    copy_zinT(k, b)
                    gelu_gate(k - 1, (b - 1) % BUFS)
                    copy_actT(k - 2, (b - 2) % BUFS)
            gelu_gate(TILES - 1, (TILES - 1) % BUFS)
            copy_actT(TILES - 2, (TILES - 2) % BUFS)
            copy_actT(TILES - 1, (TILES - 1) % BUFS)

            for g in range(GROUPS):
                ac.wait_ge(fneg_done, g + 1)
                for i in range(GROUP * g, GROUP * g + GROUP):
                    if i:
                        ac.wait_ge(fssq_done, i)
                    ac.activation(junk[:, 0, :], s2[:, i, :], ACT.Square, bias=fneg[:, i:i + 1],
                                  accum_out=fssq[:, i:i + 1]).then_inc(fssq_done, 1)

        @block.vector
        def _(ve):
            st = Steps(ve, dve_steps)
            ve.memset(zero[:, :], 0.0).then_inc(set_up, 1)
            ve.wait_ge(c_loaded, 16)
            ve.tensor_copy(tok[:, :], const("tok")).then_inc(set_up, 1)
            ve.wait_ge(wr_loaded, 32)
            ve.wait_ge(scattered, 16)
            ve.wait_ge(z_saved, 16)
            ve.tensor_scalar(w_r[:, :], w_r0[:, :], w_rs[:, 0:1], None, ALU.mult).then_inc(set_up, 1)
            st.chain(ve.tensor_copy(base[:, 0, :], const("ebase")))
            lead = st.n

            def heads(t, n=H):
                return t.rearrange("p (h e) -> p h e", e=HE)

            def features(g, j):
                n, s = GROUP * g + j, j % 2
                ve.wait_ge(act_in, 3 * (n + 1))
                if not (isinstance(g, int) and n < 2):
                    ve.wait_ge(state_done, n - 1)
                    ve.wait_ge(kv_done, n - 1)
                    ve.wait_ge(qTp_done, n - 1)
                ve.scalar_tensor_tensor(out=qk[:, s, :], in0=eqk[:, s, :], scalar=1.0, in1=rqk[:, s, :],
                                        op0=ALU.min, op1=ALU.add).then_inc(phi_done, 1)

            def mask_state(g, j):
                n, s = GROUP * g + j, j % 2
                if isinstance(g, int) and n < 1:
                    ve.wait_ge(state_zero, 1)
                else:
                    ve.wait_ge(state_done, n)
                if not (isinstance(g, int) and n < 2):
                    ve.wait_ge(inter_done, n - 1)
                ve.tensor_tensor(state_m[:, s, :], state_ps, const("block"), ALU.mult).then_inc(state_used, 1)

            def attend(g, j, between=lambda i: None):
                n, s = GROUP * g + j, j % 2
                q = qk[:, s, 0:D].rearrange("p (h d) -> p h d", d=HD)
                for b, (h0, h1) in enumerate(HEADS):
                    ve.wait_ge(pre_done, 3 * n + b + 1)
                    nh = h1 - h0
                    cols = nh * HE * HD
                    ve.tensor_tensor(
                        prod[:, h0 * HE * HD:h1 * HE * HD].rearrange("p (h e d) -> p h e d", e=HE, d=HD),
                        pre_ps[b][:, 0:cols].rearrange("p (h e d) -> p h e d", e=HE, d=HD),
                        q[:, h0:h1, :].unsqueeze(2).to_broadcast([P, nh, HE, HD]), ALU.mult).then_inc(pre_used, 1)
                    between(b)
                ve.wait_ge(pre_used, 3 * (n + 1))
                m = st.did(ve.tensor_reduce(num[:, :], prod[:, :].rearrange("p (c d) -> p c d", d=HD), AX.X, ALU.add))
                between(3)
                ve.wait_ge(inter_done, n + 1)
                st.need(m)
                ve.tensor_tensor(num2[:, :], inter_ps, num[:, :], ALU.add).then_inc(inter_used, 1)
                between(4)
                ve.wait_ge(inter_used, n + 1)
                m = st.did(ve.tensor_scalar(den[:, :], heads(num2[:, :])[:, :, HD], DEN_MIN, None, ALU.max))
                between(5)
                st.need(m)
                m = st.did(ve.reciprocal(rden[:, :], den[:, :]))
                between(6)
                st.need(m)
                if not (isinstance(g, int) and n < 2):
                    ve.wait_ge(oTp_done, n - 1)
                ve.tensor_tensor(o[:, s, :].rearrange("p (h d) -> p h d", d=HD), heads(num2[:, :])[:, :, 0:HD],
                                 rden[:, :].unsqueeze(2).to_broadcast([P, H, HD]), ALU.mult).then_inc(o_done, 1)
                ve.wait_ge(o_done, n + 1)
                between(7)

            def residual(g, j):
                n = GROUP * g + j
                ve.wait_ge(y_done, n + 1)
                ve.wait_ge(x_loaded[j], 16 * (g + 1))
                if j < 2 and not (isinstance(g, int) and g == 0):
                    ve.wait_ge(z_done, GROUP * g)
                ve.scalar_tensor_tensor(out=y[:, j, :], in0=y_ps, scalar=1.0, in1=xs[:, j, :], op0=ALU.mult,
                                        op1=ALU.add, accum_out=ysum[:, j:j + 1]).then_inc(r1_done, 1)

            def by_token(t):
                return t.unsqueeze(2).to_broadcast([P, GROUP, E])

            def tt(out, a, b, op):
                st.chain(ve.tensor_tensor(out, a, b, op))

            def mean(g):
                ve.wait_ge(r1_done, GROUP * g + GROUP)
                ve.tensor_scalar(negm[:, :], ysum[:, :], -1.0 / D, None, ALU.mult).then_inc(negm_done, 1)

            def variance(g):
                ve.wait_ge(ssq_done, GROUP * g + GROUP)
                ve.tensor_scalar(vare[:, :], ssq[:, :], 1.0 / D, LN_EPS, ALU.mult, ALU.add).then_inc(vare_done, 1)

            def shifts(g):
                ve.wait_ge(rstd_done, g + 1)
                ve.wait_ge(negm_done, g + 1)
                ve.tensor_tensor(shift[:, :], negm[:, :], rstd[:, :], ALU.mult).then_inc(shift_done, 1)

            def rms(g):
                ve.wait_ge(zsq_done, GROUP * g + GROUP)
                ve.tensor_scalar(zsqe[:, :], zsq[:, :], D * RMS_EPS, None, ALU.add).then_inc(zsqe_done, 1)

            def pick(values, top, eq, key, first, ind):
                st.chain(ve.tensor_reduce(R1[top][:, :], R[values][:, :, :], AX.X, ALU.max))
                tt(R[eq][:, :, :], R[values][:, :, :], by_token(R1[top][:, :]), ALU.is_equal)
                tt(R[key][:, :, :], R[eq][:, :, :], const("desc").rearrange("p (c e) -> p c e", e=E), ALU.mult)
                st.chain(ve.tensor_reduce(R1[first][:, :], R[key][:, :, :], AX.X, ALU.max))
                tt(R[ind][:, :, :], const("desc").rearrange("p (c e) -> p c e", e=E), by_token(R1[first][:, :]),
                   ALU.is_equal)

            def choose(g):
                ve.wait_ge(lgs_done, g + 1)
                ve.wait_ge(rrms_done, g + 1)
                tt(R["logit"][:, :, :], lgs[:, :, :], by_token(rrms[:, :]), ALU.mult)
                pick("logit", "m1", "eq1", "key1", "k1", "ind1")
                ve.tensor_tensor(R["dlog"][:, :, :], R["logit"][:, :, :], by_token(R1["m1"][:, :]),
                                 ALU.subtract).then_inc(dlog_done, 1)
                st.chain(ve.scalar_tensor_tensor(out=R["rest"][:, :, :], in0=R["ind1"][:, :, :], scalar=BELOW,
                                                 in1=R["logit"][:, :, :], op0=ALU.mult, op1=ALU.add))
                pick("rest", "m2", "eq2", "key2", "k2", "ind2")
                ve.tensor_tensor(R["ind"][:, :, :], R["ind1"][:, :, :], R["ind2"][:, :, :],
                                 ALU.add).then_inc(ind_done, 1)
                ve.wait_ge(ind_done, g + 1)

            def weigh(g):
                ve.wait_ge(elog_done, g + 1)
                st.chain(ve.tensor_reduce(R1["esum"][:, :], R["elog"][:, :, :], AX.X, ALU.add))
                st.chain(ve.reciprocal(R1["einv"][:, :], R1["esum"][:, :]))
                tt(R["prob"][:, :, :], R["elog"][:, :, :], by_token(R1["einv"][:, :]), ALU.mult)
                tt(R["gw"][:, :, :], R["prob"][:, :, :], R["ind"][:, :, :], ALU.mult)
                st.chain(ve.tensor_reduce(R1["ren"][:, :], R["gw"][:, :, :], AX.X, ALU.add))
                st.chain(ve.scalar_tensor_tensor(out=R1["reng"][:, :], in0=R1["ren"][:, :], scalar=0.0,
                                                 in1=R1["ren"][:, :], op0=ALU.is_le, op1=ALU.add))
                st.chain(ve.reciprocal(R1["renr"][:, :], R1["reng"][:, :]))
                tt(R["comb"][:, :, :], R["gw"][:, :, :], by_token(R1["renr"][:, :]), ALU.mult)
                tt(rows[:, :, D:D + E], R["comb"][:, :, :],
                   pes_b[:, :].unsqueeze(1).to_broadcast([P, GROUP, E]), ALU.mult)
                st.chain(ve.scalar_tensor_tensor(out=rows[:, :, D + E:D + 2 * E], in0=R["ind2"][:, :, :],
                                                 scalar=float(T), in1=by_token(tok[:, :]), op0=ALU.mult,
                                                 op1=ALU.add))
                st.chain(ve.tensor_scalar(tok[:, :], tok[:, :], float(GROUP * P), None, ALU.add))

            def slots(g):
                ve.wait_ge(rank_done, 2 * g + 2)
                tot = tot_ps.rearrange("p (c e) -> p c e", e=E)
                for i in range(GROUP):
                    tt(base[:, i + 1, :], tot[:, i, :], base[:, i, :], ALU.add)
                tt(R["pos"][:, :, :], rank_ps.rearrange("p (c e) -> p c e", e=E), base[:, 0:GROUP, :], ALU.add)
                tt(pos12[:, 0:GROUP, :], R["pos"][:, :, :], R["ind1"][:, :, :], ALU.mult)
                tt(pos12[:, GROUP:2 * GROUP, :], R["pos"][:, :, :], R["ind2"][:, :, :], ALU.mult)
                st.chain(ve.tensor_reduce(slot_f[:, :], pos12[:, :, :], AX.X, ALU.add))
                st.chain(ve.tensor_copy(slot[:, :], slot_f[:, :]))
                ve.tensor_copy(base[:, 0, :], base[:, GROUP, :]).then_inc(route_done, 1)
                ve.wait_ge(route_done, g + 1)

            def body(g, first):
                st.start(lead if first else lead + FIRST_STEPS + (g - 1) * BODY_STEPS)
                for j in range(GROUP):
                    features(g, j)
                    if not first and j == 2:
                        variance(g - 1)
                    if j >= 1:
                        mask_state(g, j - 1)
                        attend(g, j - 1)
                    elif not first:
                        mask_state(g - 1, GROUP - 1)
                        attend(g - 1, GROUP - 1)
                    if not first and j == 2:
                        shifts(g - 1)
                    if not first and j == 3:
                        rms(g - 1)
                    if j >= 2:
                        residual(g, j - 2)
                    elif not first:
                        residual(g - 1, GROUP - 2 + j)
                    if not first and j == 1:
                        mean(g - 1)
                    if not first and j == 3:
                        choose(g - 1)
                        weigh(g - 1)
                        slots(g - 1)
                assert st.n == (FIRST_STEPS if first else BODY_STEPS), st.n

            FIRST_STEPS = 3 * (GROUP - 1)
            BODY_STEPS = 3 * GROUP + 12 + 11 + 9
            groups(ve, body)
            last = GROUPS - 1
            st.start(lead + FIRST_STEPS + (GROUPS - 1) * BODY_STEPS)
            mask_state(last, GROUP - 1)
            attend(last, GROUP - 1)
            residual(last, GROUP - 2)
            residual(last, GROUP - 1)
            mean(last)
            variance(last)
            shifts(last)
            rms(last)
            choose(last)
            weigh(last)
            slots(last)

            ve.tensor_copy(cnt_i[:, :], base[:, 0, :]).then_inc(cnt_done, 1)
            st.chain(ve.scalar_tensor_tensor(out=nt_f[:, :], in0=base[:, 0, :], scalar=float(P - 1),
                                             in1=const("ebase"), op0=ALU.add, op1=ALU.subtract))
            st.chain(ve.tensor_copy(nt_i[:, :], nt_f[:, :]))
            st.chain(ve.tensor_scalar(nt_s[:, :], nt_i[:, :], P.bit_length() - 1, None, ALU.arith_shift_right))
            st.chain(ve.tensor_copy(ntile[:, :], nt_s[:, :]))
            cum = ntile
            for step, nxt in ((1, cumA), (2, cumB), (4, cumC)):
                m1 = st.did(ve.tensor_copy(nxt[:, 0:step], cum[:, 0:step]))
                m2 = st.did(ve.tensor_tensor(nxt[:, step:E], cum[:, step:E], cum[:, 0:E - step], ALU.add))
                st.need(m2)
                cum = nxt
            st.chain(ve.tensor_scalar(skip[:, :], ntile[:, :], float(-P), float(REGION), ALU.mult, ALU.add))
            a, b = CONST["tile"]
            num_t = C[0:1, a:b]
            tt(past[:, :, :], cum[0:1, :].unsqueeze(1).to_broadcast([1, TILES, E]),
               num_t.unsqueeze(2).to_broadcast([1, TILES, E]), ALU.is_le)
            tt(pskip[:, :, :], past[:, :, :], skip[0:1, :].unsqueeze(1).to_broadcast([1, TILES, E]), ALU.mult)
            st.chain(ve.tensor_reduce(te_f[:, :], past[:, :, :], AX.X, ALU.add))
            st.chain(ve.tensor_reduce(tr_f[:, :], pskip[:, :, :], AX.X, ALU.add))
            st.chain(ve.tensor_scalar(tile_e[:, :], te_f[:, :], float(E - 1), None, ALU.min))
            st.chain(ve.scalar_tensor_tensor(out=tr_g[:, :], in0=num_t, scalar=float(P), in1=tr_f[:, :],
                                             op0=ALU.mult, op1=ALU.add))
            ve.tensor_copy(tile_r[:, :], tr_g[:, :]).then_inc(table_done, 1)
            ve.wait_ge(table_done, 1)

            expert = ve.alloc_register("expert_v")

            def meta(k, b, rnd):
                ve.reg_load(expert, tile_e[0:1, bass.ds(k, 1)] if not isinstance(k, int) else tile_e[0:1, k:k + 1])
                ex = ve.snap(expert, min_val=0, max_val=E - 1)
                ve.wait_ge(zin_loaded[b], 16 * (rnd + 1))
                ve.wait_ge(zinTp_done, k + 1)
                if not (isinstance(k, int) and k < BUFS):
                    ve.wait_ge(act_done, k - BUFS + 1)
                    ve.wait_ge(placed[b], 16 * rnd)
                ve.tensor_copy(wcol[:, b:b + 1], zin[:, b, bass.ds(ex + D, 1)]).then_inc(meta_done, 1)
                ve.tensor_copy(dst[:, b:b + 1], zin[:, b, bass.ds(ex + D + E, 1)]).then_inc(meta_done, 1)

            def activate(k, b):
                ve.wait_ge(gelu_done, k + 1)
                ve.wait_ge(gate_done, k + 1)
                ve.wait_ge(meta_done, 2 * (k + 1))
                ve.scalar_tensor_tensor(out=act[:, b, :], in0=gelu[:, b, :], scalar=wcol[:, b:b + 1],
                                        in1=gate_ps[b][:, HID:2 * HID], op0=ALU.mult, op1=ALU.mult)\
                  .then_inc(act_done, 1)

            def take(k, b):
                ve.wait_ge(yp_done, k + 1)
                ve.tensor_copy(yout[:, b, :], yout_ps).then_inc(yout_done, 1)

            meta(0, 0, 0)
            meta(1, 1, 0)
            activate(0, 0)
            meta(2, 2, 0)
            activate(1, 1)
            take(0, 0)
            with ve.Fori(1, TILES // BUFS) as i:
                for b in range(BUFS):
                    k = BUFS * i + b
                    meta(k, b, i)
                    activate(k - 1, (b - 1) % BUFS)
                    take(k - 2, (b - 2) % BUFS)
            activate(TILES - 1, (TILES - 1) % BUFS)
            take(TILES - 2, (TILES - 2) % BUFS)
            take(TILES - 1, (TILES - 1) % BUFS)

            ve.wait_ge(z_saved, 16 * (GROUPS + 1))

            def total(g):
                c = slice(GROUP * g, GROUP * g + GROUP)
                ve.wait_ge(pl_loaded[g], 32)
                tt(s1[:, c, :], pl[:, 0, c, :], pl[:, 1, c, :], ALU.add)
                for i in range(GROUP * g, GROUP * g + GROUP):
                    ve.scalar_tensor_tensor(out=s2[:, i, :], in0=s1[:, i, :], scalar=1.0, in1=zall[:, i, :],
                                            op0=ALU.mult, op1=ALU.add,
                                            accum_out=fsum[:, i:i + 1]).then_inc(fsum_done, 1)
                ve.wait_ge(fsum_done, GROUP * (g + 1))
                ve.tensor_scalar(fneg[:, c], fsum[:, c], -1.0 / D, None, ALU.mult).then_inc(fneg_done, 1)

            def scale(g):
                c = slice(GROUP * g, GROUP * g + GROUP)
                ve.wait_ge(fssq_done, GROUP * (g + 1))
                ve.tensor_scalar(fvar[:, c], fssq[:, c], 1.0 / D, LN_EPS, ALU.mult, ALU.add).then_inc(fvar_done, 1)

            def finish(g):
                ve.wait_ge(frs_done, g + 1)
                for i in range(GROUP * g, GROUP * g + GROUP):
                    ve.tensor_scalar(res[:, i, :], s2[:, i, :], fneg[:, i:i + 1], frs[:, i:i + 1], ALU.add,
                                     ALU.mult).then_inc(res_done, 1)

            total(0)
            for g in range(1, GROUPS):
                total(g)
                scale(g - 1)
                if g >= 2:
                    finish(g - 2)
            ve.wait_ge(fneg_done, GROUPS)
            scale(GROUPS - 1)
            finish(GROUPS - 2)
            finish(GROUPS - 1)


def constants():
    import numpy as np

    c = np.zeros((P, NCONST), np.float32)
    i = np.arange(P)

    def put(name, v):
        a, b = CONST[name]
        c[:, a:b] = v

    put("tri", i[:, None] <= i[None, :])
    put("stri", i[:, None] < i[None, :])
    put("ident", np.eye(P))
    put("ones", 1.0)
    put("block", (i[:, None] // HD) == (np.arange(H * HE)[None, :] // HE))
    put("desc", np.tile(E - np.arange(E), GROUP)[None, :])
    put("tok", i[:, None] + P * np.arange(GROUP)[None, :])
    put("ebase", (np.arange(E) * REGION)[None, :])
    put("tile", np.arange(TILES)[None, :])
    put("half", -0.5)
    put("pad", K * T + i[:, None] + P * np.arange(PADS)[None, :])
    return c


def kernel(**inputs):
    import numpy as np
    import concourse.bacc as bacc
    from concourse.bass_utils import run_bass_kernel_spmd

    a = {k: np.asarray(v) for k, v in inputs.items()}
    x = a["L0_attn_x"].reshape(T, D)
    wqkv = np.concatenate([a["L0_attn_Wq"].T, a["L0_attn_Wk"].T, a["L0_attn_Wv"].T], axis=1)
    arrays = {
        "xT": x.T,
        "x": x,
        "wqkv": wqkv,
        "wo": a["L0_attn_Wo"].T,
        "rw": a["L0_ffn_router_w"],
        "rscale": a["L0_ffn_router_scale"].reshape(D, 1),
        "pes": np.broadcast_to(a["L0_ffn_per_expert_scale"].reshape(1, E), (P, E)),
        "gate_w": a["L0_ffn_gating_w"].transpose(3, 0, 1, 2).reshape(D, E * 2 * HID),
        "lin_w": a["L0_ffn_linear_w"].reshape(E, HB, P, D).transpose(2, 0, 1, 3).reshape(P, E * HB * D),
        "consts": constants(),
    }
    arrays = {k: np.ascontiguousarray(v) for k, v in arrays.items()}
    nc = bacc.Bacc("TRN2", target_bir_lowering=False, num_devices=1)
    args = [nc.dram_tensor("in_" + k, v.shape, F32, kind="ExternalInput").ap() for k, v in arrays.items()]
    out = nc.dram_tensor("out_0", (T, D), F32, kind="ExternalOutput").ap()
    build(nc, *args, out)
    r = run_bass_kernel_spmd(nc, [{"in_" + k: v for k, v in arrays.items()}], core_ids=[0])
    return r.results[0]["out_0"].reshape(1, T, D)
```

```python
from contextlib import ExitStack

import concourse.bass as bass
from concourse import mybir
from concourse.alu_op_type import AluOpType as ALU

F32 = mybir.dt.float32
I32 = mybir.dt.int32
U32 = mybir.dt.uint32
ACT = mybir.ActivationFunctionType
AX = mybir.AxisListType

P = 128
D = 128
T = 2048
CHUNKS = T // P
GROUP = 4
GROUPS = CHUNKS // GROUP
H, HD = 16, 8
HE = HD + 1
KV = H * HE * HD
HEADS = [(0, 6), (6, 12), (12, 16)]
E, K, HID = 8, 2, 256
HB = HID // P
REGION = T + P
SPARE = E * REGION
BUFS = 8
FULL = T * K // P
TILES = -(-(FULL + E - 1) // BUFS) * BUFS
NSPARE = TILES - FULL
PADS = E + NSPARE
ROW = D + 2
EW = (2 + 1) * HID
LN_EPS, RMS_EPS, DEN_MIN = 1e-5, 1e-6, 1e-6
BELOW = -3.0e38

CONST = {}
_at = 0
for _name, _n in (("tri", P), ("stri", P), ("ident", P), ("ones", P), ("block", H * HE), ("desc", GROUP * E),
                  ("tok", K * GROUP), ("ebase", E), ("tile", TILES), ("half", GROUP), ("pad", PADS)):
    CONST[_name] = (_at, _at + _n)
    _at += _n
NCONST = _at



class Steps:

    def __init__(self, eng, sem):
        self.eng, self.sem, self.base, self.n = eng, sem, 0, 0

    def start(self, base):
        self.base, self.n = base, 0

    def ready(self, last=0):
        self.eng.wait_ge(self.sem, self.base + self.n - last)

    def did(self, ins):
        ins.then_inc(self.sem, 1)
        self.n += 1

    def chain(self, ins):
        self.did(ins)
        self.ready()


def build(nc, xT, x, wqkv, wo, rw, rscale, pes, expert_w, consts, out):
    zbuf = nc.dram_tensor("zbuf", (SPARE + NSPARE * P, ROW), F32, kind="Internal").ap()
    planes = nc.dram_tensor("planes", (K * T + PADS * P, D), F32, kind="Internal").ap()

    with ExitStack() as ctx:
        def sb(name, shape, dt=F32):
            return ctx.enter_context(nc.sbuf_tensor(name, shape, dt))

        def bank(name, shape):
            return ctx.enter_context(nc.psum_tensor(name, shape, F32))

        def sem(name):
            return ctx.enter_context(nc.semaphore(name))

        C = sb("C", [P, NCONST])

        def const(name):
            a, b = CONST[name]
            return C[:, a:b]

        w_qkv = sb("w_qkv", [P, 3 * D])
        w_o = sb("w_o", [P, D])
        w_r0 = sb("w_r0", [P, E])
        w_rs = sb("w_rs", [P, 1])
        w_r = sb("w_r", [P, E])
        pes_b = sb("pes_b", [P, E])
        w_e = sb("w_e", [P, E * EW])
        xTs = sb("xTs", [P, GROUP, P])
        xs = sb("xs", [P, CHUNKS, D])
        eqk = sb("eqk", [P, 2, 2 * D])
        rqk = sb("rqk", [P, 2, 2 * D])
        qk = sb("qk", [P, GROUP, 2 * D])
        v1 = sb("v1", [P, GROUP, H * HE])
        kv = sb("kv", [P, GROUP, KV])
        prod = sb("prod", [P, KV])
        num = sb("num", [P, H * HE])
        num2 = sb("num2", [P, H * HE])
        den = sb("den", [P, H])
        rden = sb("rden", [P, H])
        o = sb("o", [P, 2, D])
        qT = sb("qT", [P, 2, P])
        oT = sb("oT", [P, 2, P])
        state_m = sb("state_m", [P, 2, H * HE])
        pads = sb("pads", [P, PADS, ROW])
        zero = sb("zero", [P, H * HE])
        y = sb("y", [P, GROUP + 1, D])
        zs = sb("zs", [P, GROUP, D])
        junk = sb("junk", [P, 2, D])
        rows = sb("rows", [P, GROUP, K, ROW])
        zT = sb("zT", [P, GROUP, P])
        lgs = sb("lgs", [P, GROUP, E])
        ysum = sb("ysum", [P, GROUP])
        negm = sb("negm", [P, GROUP])
        ssq = sb("ssq", [P, GROUP])
        vare = sb("vare", [P, GROUP])
        rstd = sb("rstd", [P, GROUP])
        shift = sb("shift", [P, GROUP])
        zsq = sb("zsq", [P, GROUP])
        zsqe = sb("zsqe", [P, GROUP])
        rrms = sb("rrms", [P, GROUP])
        names = ["logit", "eq1", "key1", "rest", "eq2", "key2", "dlog", "elog", "prob", "ind", "gw", "comb", "combs",
                 "pos"]
        R = {n: sb("r_" + n, [P, GROUP, E]) for n in names}
        names1 = ["m1", "k1", "m2", "k2", "esum", "einv", "ren", "reng", "renr"]
        R1 = {n: sb("r_" + n, [P, GROUP]) for n in names1}
        ind12 = sb("ind12", [P, K, GROUP, E])
        R["ind1"], R["ind2"] = ind12[:, 0], ind12[:, 1]
        comb12 = sb("comb12", [P, K, GROUP, E])
        tok = sb("tok", [P, K * GROUP])
        rank = sb("rank", [P, 2, GROUP, E])
        base = sb("base", [P, GROUP + 1, E])
        pos12 = sb("pos12", [P, K, GROUP, E])
        slot_f = sb("slot_f", [P, K * GROUP])
        slot = sb("slot", [P, K * GROUP], I32)
        cnt_i = sb("cnt_i", [P, E], I32)
        nt_f = sb("nt_f", [P, E])
        nt_i = sb("nt_i", [P, E], I32)
        nt_s = sb("nt_s", [P, E], I32)
        ntile = sb("ntile", [P, E])
        cumA = sb("cumA", [P, E])
        cumB = sb("cumB", [P, E])
        cumC = sb("cumC", [P, E])
        skip = sb("skip", [P, E])
        past = sb("past", [1, TILES, E])
        pskip = sb("pskip", [1, TILES, E])
        te_f = sb("te_f", [1, TILES])
        tr_f = sb("tr_f", [1, TILES])
        tr_g = sb("tr_g", [1, TILES])
        te_g = sb("te_g", [1, TILES])
        tile_w = sb("tile_w", [1, TILES], I32)
        tile_r = sb("tile_r", [1, TILES], I32)
        zin = sb("zin", [P, BUFS, ROW])
        zinT = sb("zinT", [P, 2, P])
        gelu = sb("gelu", [P, 2, HID])
        act = sb("act", [P, 2, HID])
        actT = sb("actT", [P, 2, HB, P])
        yout = sb("yout", [P, BUFS, D])
        zall = sb("zall", [P, CHUNKS, D])
        pl = sb("pl", [P, K, CHUNKS, D])
        s1 = sb("s1", [P, CHUNKS, D])
        s2 = sb("s2", [P, CHUNKS, D])
        fsum = sb("fsum", [P, CHUNKS])
        fneg = sb("fneg", [P, CHUNKS])
        fssq = sb("fssq", [P, CHUNKS])
        fvar = sb("fvar", [P, CHUNKS])
        frs = sb("frs", [P, CHUNKS])
        fshift = sb("fshift", [P, CHUNKS])
        res = sb("res", [P, CHUNKS, D])

        B = [bank(f"bank{i}", [P, 512]) for i in range(8)]
        qkv_ps = B[0]
        pre_ps = B[2:5]
        state_ps = B[5][:, 0:H * HE]
        turn_ps = B[1]
        qT_ps, oT_ps = B[1][:, 0:P], B[1][:, P:2 * P]
        inter_ps, rank_ps = B[6][:, 0:H * HE], B[6][:, 256:256 + 2 * GROUP * E]
        y_ps, lg_ps = B[7][:, 0:D], B[7][:, 256:256 + GROUP * E]
        gate_ps, zinT_ps, actT_ps, yout_ps = B[0:2], B[2:4], B[4:6], B[6:8]

        w_loaded = sem("w_loaded")
        c_loaded = sem("c_loaded")
        wr_loaded = sem("wr_loaded")
        we_loaded = sem("we_loaded")
        xT_loaded = [sem(f"xT_loaded{j}") for j in range(GROUP)]
        x_loaded = sem("x_loaded")
        set_up = sem("set_up")
        pool_set_up = sem("pool_set_up")
        state_zero = sem("state_zero")
        qkv_done = sem("qkv_done")
        act_in = sem("act_in")
        phi_done = sem("phi_done")
        kv_done = sem("kv_done")
        qTp_done = sem("qTp_done")
        qT_done = sem("qT_done")
        pre_done = sem("pre_done")
        pre_used = sem("pre_used")
        state_used = sem("state_used")
        inter_done = sem("inter_done")
        state_done = sem("state_done")
        inter_used = sem("inter_used")
        o_done = sem("o_done")
        oTp_done = sem("oTp_done")
        oT_done = sem("oT_done")
        y_done = sem("y_done")
        summed = sem("summed")
        den_done = sem("den_done")
        rden_done = sem("rden_done")
        y_used = sem("y_used")
        negm_done = sem("negm_done")
        ssq_done = sem("ssq_done")
        vare_done = sem("vare_done")
        rstd_done = sem("rstd_done")
        shift_done = sem("shift_done")
        z_done = sem("z_done")
        zsq_done = sem("zsq_done")
        zTp_done = sem("zTp_done")
        zT_done = sem("zT_done")
        lg_done = sem("lg_done")
        lgs_done = sem("lgs_done")
        zsqe_done = sem("zsqe_done")
        rrms_done = sem("rrms_done")
        dlog_done = sem("dlog_done")
        elog_done = sem("elog_done")
        ind_done = sem("ind_done")
        rank_done = sem("rank_done")
        rank_used = sem("rank_used")
        y_moved = sem("y_moved")
        rows_done = sem("rows_done")
        route_done = sem("route_done")
        scattered = sem("scattered")
        z_saved = sem("z_saved")
        cnt_done = sem("cnt_done")
        table_done = sem("table_done")
        padded = sem("padded")
        zin_loaded = [sem(f"zin_loaded{j}") for j in range(BUFS)]
        zinTp_done = sem("zinTp_done")
        zinT_done = sem("zinT_done")
        gate_done = sem("gate_done")
        gelu_done = sem("gelu_done")
        act_done = sem("act_done")
        actTp_done = sem("actTp_done")
        actT_done = sem("actT_done")
        yp_done = sem("yp_done")
        yout_done = sem("yout_done")
        placed = [sem(f"placed{j}") for j in range(BUFS)]
        pl_loaded = [sem(f"pl_loaded{g}") for g in range(GROUPS)]
        fsum_done = sem("fsum_done")
        fneg_done = sem("fneg_done")
        fssq_done = sem("fssq_done")
        fvar_done = sem("fvar_done")
        frs_done = sem("frs_done")
        fshift_done = sem("fshift_done")
        res_done = sem("res_done")
        stored = sem("stored")
        pads_done = sem("pads_done")
        scatter_go = sem("scatter_go")
        dve_steps = sem("dve_steps")

        def exists(g, m):
            return not isinstance(g, int) or 0 <= GROUP * g + m < CHUNKS

        def groups(eng, step, start=lambda g: None):
            for m in range(-2, 2):
                step(0, m, None)
            for m in range(2, 6):
                step(0, m, None)
            with eng.Fori(1, GROUPS - 1) as g:
                start(g)
                for m in range(2, 6):
                    step(g, m, m - 2)
            start(GROUPS - 1)
            for m in range(2, 6):
                step(GROUPS - 1, m, m - 2)

        def at(k):
            return slice(k, k + 1) if isinstance(k, int) else bass.ds(k, 1)

        def after(eng, signal, count):
            if not (isinstance(count, int) and count <= 0):
                eng.wait_ge(signal, count)

        def tiles(eng, *stages):
            *stages, order = stages

            def step(k, b, rnd):
                for lag in order:
                    if isinstance(k, int) and not 0 <= k - lag < TILES:
                        continue
                    if isinstance(k, int):
                        stages[lag](k - lag, (k - lag) % BUFS, (k - lag) // BUFS)
                    else:
                        stages[lag](k - lag, (b - lag) % BUFS, rnd if b >= lag else rnd - 1)

            for k in range(BUFS):
                step(k, k, 0)
            with eng.Fori(1, TILES // BUFS) as i:
                for b in range(BUFS):
                    step(BUFS * i + b, b, i)
            for k in range(TILES, TILES + max(order)):
                step(k, k % BUFS, k // BUFS)

        block = ctx.enter_context(nc.Block())

        @block.sync
        def _(sp):
            sp.dma_start(w_qkv[:, :], wqkv).then_inc(w_loaded, 16)
            for j in range(GROUP):
                sp.dma_start(xTs[:, j, :], xT[:, j * P:(j + 1) * P]).then_inc(xT_loaded[j], 16)
                if j == 0:
                    sp.dma_start(C[:, :], consts).then_inc(c_loaded, 16)
            sp.dma_start(xs[:, :, :], x.rearrange("(c p) d -> p c d", p=P)).then_inc(x_loaded, 16)
            sp.dma_start(w_o[:, :], wo).then_inc(wr_loaded, 16)
            sp.dma_start(w_rs[:, :], rscale).then_inc(z_saved, 16)
            sp.dma_start(pes_b[:, :], pes).then_inc(wr_loaded, 16)
            sp.dma_start(w_e[:, :], expert_w).then_inc(we_loaded, 16)

            def save_z(g):
                sp.wait_ge(z_done, GROUP * g + GROUP)
                sp.dma_start(zall[:, bass.ds(GROUP * g, GROUP), :], zs[:, :, :]).then_inc(z_saved, 16)

            def load(g):
                for j in range(GROUP):
                    n = GROUP * g + j
                    sp.wait_ge(qkv_done, n - GROUP + 1)
                    sp.dma_start(xTs[:, j, :], xT[:, bass.ds(n * P, P)]).then_inc(xT_loaded[j], 16)
                if not isinstance(g, int):
                    save_z(g - 2)

            load(1)
            with sp.Fori(2, GROUPS) as g:
                load(g)
            save_z(GROUPS - 2)
            save_z(GROUPS - 1)

            sp.wait_ge(cnt_done, 1)
            sp.wait_ge(pads_done, 1)
            end = sp.alloc_register("rows_end")
            for e in range(E):
                sp.reg_load(end, cnt_i[0:1, e:e + 1])
                at = sp.snap(end, min_val=0, max_val=SPARE - P)
                sp.dma_start(zbuf[bass.ds(at, P), :], pads[:, e, :]).then_inc(padded, 16)
            sp.dma_start(zbuf[SPARE:, :].rearrange("(b p) r -> p b r", p=P), pads[:, E:, :]).then_inc(padded, 16)
            sp.wait_ge(table_done, 1)
            sp.wait_ge(padded, 16 * (E + 1))
            sp.wait_ge(scattered, 16 * (K * CHUNKS + 1))
            row = sp.alloc_register("tile_row")
            for b in range(BUFS):
                sp.reg_load(row, tile_r[0:1, b:b + 1])
                at = sp.snap(row, min_val=0, max_val=SPARE + (NSPARE - 1) * P)
                sp.dma_start(zin[:, b, :], zbuf[bass.ds(at, P), :]).then_inc(zin_loaded[b], 16)
            with sp.Fori(1, TILES // BUFS) as i:
                for b in range(BUFS):
                    k = BUFS * i + b
                    sp.reg_load(row, tile_r[0:1, bass.ds(k, 1)])
                    at = sp.snap(row, min_val=0, max_val=SPARE + (NSPARE - 1) * P)
                    sp.wait_ge(placed[b], 16 * i)
                    sp.dma_start(zin[:, b, :], zbuf[bass.ds(at, P), :]).then_inc(zin_loaded[b], 16)
            for b in range(BUFS):
                sp.wait_ge(placed[b], 16 * (TILES // BUFS))
            for g in range(GROUPS):
                for k in range(K):
                    at = k * T + g * GROUP * P
                    sp.dma_start(pl[:, k, g * GROUP:(g + 1) * GROUP, :],
                                 planes[at:at + GROUP * P, :].rearrange("(c p) d -> p c d", p=P))\
                      .then_inc(pl_loaded[g], 16)
            for g in range(GROUPS):
                sp.wait_ge(res_done, GROUP * (g + 1))
                sp.dma_start(out[g * GROUP * P:(g + 1) * GROUP * P, :].rearrange("(c p) d -> p c d", p=P),
                             res[:, g * GROUP:(g + 1) * GROUP, :]).then_inc(stored, 16)
            sp.wait_ge(stored, 16 * GROUPS)

        @block.gpsimd
        def _(pool):
            pool.dma_start(w_r0[:, :], rw).then_inc(scattered, 16)
            pool.memset(v1[:, :, :], 1.0).then_inc(pool_set_up, 1)
            pool.memset(pads[:, :, :], 0.0).then_inc(pool_set_up, 1)
            pool.wait_ge(c_loaded, 16)
            pool.wait_ge(pool_set_up, 2)
            pool.tensor_copy(pads[:, :, D + 1].bitcast(I32), const("pad"))\
                .then_inc(pads_done, 1)

            def outer(g, m):
                n, s = GROUP * g + m, m % GROUP
                pool.wait_ge(phi_done, n + 1)
                after(pool, pre_done, 3 * (n - GROUP + 1))
                a = v1[:, s, :].rearrange("p (h e) -> p h e", e=HE).unsqueeze(3).to_broadcast([P, H, HE, HD])
                b = qk[:, s, D:2 * D].rearrange("p (h d) -> p h d", d=HD).unsqueeze(2).to_broadcast([P, H, HE, HD])
                pool.tensor_tensor(kv[:, s, :].rearrange("p (h e d) -> p h e d", e=HE, d=HD), a, b,
                                   ALU.mult).then_inc(kv_done, 1)

            def norm_pow(g):
                pool.wait_ge(vare_done, g + 1)
                pool.tensor_tensor(rstd[:, :], vare[:, :], const("half"), ALU.pow).then_inc(rstd_done, 1)

            def rms_pow(g):
                pool.wait_ge(zsqe_done, g + 1)
                pool.tensor_tensor(rrms[:, :], zsqe[:, :], const("half"), ALU.pow).then_inc(rrms_done, 1)

            def scatter(g, part=range(GROUP)):
                pool.wait_ge(route_done, g + 1)
                pool.wait_ge(rows_done, GROUP * g + GROUP)
                for j in part:
                    for r in range(K):
                        c = r * GROUP + j
                        pool.indirect_dma_start(
                            zbuf, bass.IndirectOffsetOnAxis(ap=slot[:, c:c + 1].bitcast(U32), axis=0),
                            rows[:, j, r, :], None).then_inc(scattered, 16)

            def step(g, m, route):
                if route == 0:
                    norm_pow(g - 1)
                if route == 2:
                    rms_pow(g - 1)
                if exists(g, m + 2):
                    outer(g, m + 2)
                if route is not None and g >= 2:
                    scatter(g - 2, ((0,), (1, 2), (3,), ())[route])

            for m in range(-2, 2):
                step(0, m, None)
            for g in range(GROUPS):
                for m in range(2, 6):
                    step(g, m, m - 2 if g else None)
            last = GROUPS - 1
            scatter(last - 1, (0,))
            norm_pow(last)
            scatter(last - 1, (1, 2))
            rms_pow(last)
            scatter(last - 1, (3,))
            scatter(last)

            def place(k, b):
                pool.wait_ge(yout_done, k + 1)
                pool.sem_inc(scatter_go, 1)
                pool.indirect_dma_start(
                    planes, bass.IndirectOffsetOnAxis(ap=zin[:, b, D + 1:D + 2].bitcast(U32), axis=0),
                    yout[:, b, :], None).then_inc(placed[b], 16)

            with pool.Fori(0, TILES // BUFS) as i:
                for b in range(BUFS):
                    place(BUFS * i + b, b)
            for g in range(GROUPS):
                c = slice(GROUP * g, GROUP * g + GROUP)
                pool.wait_ge(fvar_done, g + 1)
                pool.tensor_tensor(frs[:, c], fvar[:, c], const("half"), ALU.pow).then_inc(frs_done, 1)

        @block.tensor
        def _(pe):
            def project(g, m):
                n = GROUP * g + m
                pe.wait_ge(xT_loaded[m % GROUP], 16 * (g + m // GROUP + 1))
                after(pe, act_in, 3 * n)
                pe.matmul(qkv_ps[:, 0:3 * D], xTs[:, m % GROUP, :], w_qkv[:, :], start=True, stop=True)\
                  .then_inc(qkv_done, 1)

            def prefix(g, m, routed):
                n, s = GROUP * g + m, m % GROUP
                pe.wait_ge(phi_done, n + 1)
                after(pe, oT_done, n - 1)
                if routed:
                    pe.wait_ge(zT_done, g)
                pe.transpose(qT_ps, qk[:, s, 0:D], const("ident")).then_inc(qTp_done, 1)
                pe.wait_ge(kv_done, n + 1)
                for b, (h0, h1) in enumerate(HEADS):
                    after(pe, pre_used, 3 * (n - 1) + b + 1 if not isinstance(g, int) or n else 0)
                    c0, c1 = h0 * HE * HD, h1 * HE * HD
                    pe.matmul(pre_ps[b][:, 0:c1 - c0], const("tri"), kv[:, s, c0:c1], start=True, stop=True)\
                      .then_inc(pre_done, 1)

            def state(g, m, ranked):
                n, s = GROUP * g + m, m % GROUP
                pe.wait_ge(state_used, n + 1)
                pe.matmul(state_ps, qk[:, s, D:2 * D], v1[:, s, :], start=False, stop=False,
                          skip_group_check=True).then_inc(state_done, 1)
                pe.wait_ge(qT_done, n + 1)
                after(pe, inter_used, n)
                if ranked:
                    pe.wait_ge(rank_used, g)
                pe.matmul(inter_ps, qT[:, m % 2, :], state_m[:, m % 2, :], start=True, stop=True)\
                  .then_inc(inter_done, 1)

            def turn_o(g, m):
                n = GROUP * g + m
                pe.wait_ge(o_done, n + 1)
                pe.wait_ge(qT_done, n + 2 if exists(g, m + 1) else CHUNKS)
                pe.transpose(oT_ps, o[:, m % 2, :], const("ident")).then_inc(oTp_done, 1)

            def put_out(g, m, routed):
                n = GROUP * g + m
                pe.wait_ge(oT_done, n + 1)
                after(pe, y_used, n)
                if routed:
                    pe.wait_ge(lgs_done, g)
                pe.matmul(y_ps, oT[:, m % 2, :], w_o[:, :], start=True, stop=False)
                pe.matmul(y_ps, const("ident"), xs[:, at(n), :].rearrange("p c d -> p (c d)"), start=False, stop=True).then_inc(y_done, 1)

            def turn_z(g):
                pe.wait_ge(z_done, GROUP * g + GROUP)
                for i in range(GROUP):
                    t = pe.transpose(turn_ps[:, i * P:(i + 1) * P], zs[:, i, :], const("ident"))
                t.then_inc(zTp_done, 1)

            def logits(g):
                pe.wait_ge(zT_done, g + 1)
                for i in range(GROUP):
                    t = pe.matmul(lg_ps[:, E * i:E * i + E], zT[:, i, :], w_r[:, :], start=True, stop=True)
                t.then_inc(lg_done, 1)

            def ranks(g):
                pe.wait_ge(ind_done, g + 1)
                flat = R["ind"][:, :, :].rearrange("p c e -> p (c e)")
                n = GROUP * E
                pe.matmul(rank_ps[:, 0:n], const("stri"), flat, start=True, stop=True).then_inc(rank_done, 1)
                pe.matmul(rank_ps[:, n:2 * n], const("ones"), flat, start=True, stop=True).then_inc(rank_done, 1)

            pe.wait_ge(c_loaded, 16)
            pe.wait_ge(set_up, 3)
            pe.wait_ge(pool_set_up, 2)
            pe.matmul(state_ps, zero[:, 0:P], zero[:, :], start=True, stop=False, skip_group_check=True)\
              .then_inc(state_zero, 1)
            pe.wait_ge(w_loaded, 16)
            pe.wait_ge(x_loaded, 16)
            pe.wait_ge(wr_loaded, 32)

            def step(g, m, route):
                if exists(g, m + 2):
                    project(g, m + 2)
                if exists(g, m - 1):
                    prefix(g, m - 1, route == 2)
                if exists(g, m - 2):
                    turn_o(g, m - 2)
                if route == 3:
                    pe.wait_ge(inter_used, GROUP * g + m - 1 if exists(g, m - 2) else CHUNKS)
                    ranks(g - 1)
                if exists(g, m - 1):
                    state(g, m - 1, route == 3)
                if route == 2:
                    pe.wait_ge(y_used, GROUP * g + m - 2 if exists(g, m - 3) else CHUNKS)
                    logits(g - 1)
                if route == 1:
                    pe.wait_ge(oT_done, GROUP * g + m - 1)
                    turn_z(g - 1)
                if exists(g, m - 2):
                    put_out(g, m - 2, route == 2)

            groups(pe, step)
            last = GROUPS - 1
            turn_z(last)
            logits(last)
            ranks(last)

            weights = [pe.alloc_register(f"weights{b}") for b in range(4)]

            def turn_in(k, b, rnd):
                pe.wait_ge(zin_loaded[b], 16 * (rnd + 1))
                after(pe, zinT_done, k - 1)
                pe.transpose(zinT_ps[b % 2][:, 0:P], zin[:, b, 0:D], const("ident")).then_inc(zinTp_done, 1)

            def gates(k, b):
                pe.reg_load(weights[b % 4], tile_w[0:1, at(k)])
                w = pe.snap(weights[b % 4], min_val=0, max_val=(E - 1) * EW)
                pe.wait_ge(zinT_done, k + 1)
                after(pe, act_done, k - 1)
                pe.matmul(gate_ps[b % 2][:, :], zinT[:, b % 2, :], w_e[:, bass.ds(w, 2 * HID)],
                          start=True, stop=True).then_inc(gate_done, 1)

            def output(k, b):
                w = pe.snap(weights[b % 4], min_val=0, max_val=(E - 1) * EW)
                pe.wait_ge(actT_done, k + 1)
                after(pe, yout_done, k - 1)
                for h in range(HB):
                    mm = pe.matmul(yout_ps[b % 2][:, 0:D], actT[:, b % 2, h, :],
                                   w_e[:, bass.ds(w + (2 * HID + h * D), D)], start=(h == 0), stop=(h == HB - 1))
                mm.then_inc(yp_done, 1)

            def turn_act(k, b):
                pe.wait_ge(act_done, k + 1)
                after(pe, actT_done, k - 1)
                for h in range(HB):
                    mm = pe.transpose(actT_ps[b % 2][:, h * P:(h + 1) * P], act[:, b % 2, h * P:(h + 1) * P],
                                      const("ident"))
                mm.then_inc(actTp_done, 1)

            pe.wait_ge(we_loaded, 16)
            pe.wait_ge(table_done, 1)
            pe.wait_ge(route_done, GROUPS)
            tiles(pe, lambda k, b, rnd: turn_in(k, b, rnd), lambda k, b, rnd: gates(k, b),
                  lambda k, b, rnd: turn_act(k, b), lambda k, b, rnd: output(k, b), (0, 1, 3, 2))

        @block.scalar
        def _(ac):
            def inputs(g, m):
                n = GROUP * g + m
                ac.wait_ge(qkv_done, n + 1)
                after(ac, phi_done, n - 1)
                ac.activation(eqk[:, m % 2, :], qkv_ps[:, 0:2 * D], ACT.Exp).then_inc(act_in, 1)
                ac.activation(rqk[:, m % 2, :], qkv_ps[:, 0:2 * D], ACT.Relu).then_inc(act_in, 1)
                after(ac, state_done, n - GROUP + 1)
                after(ac, kv_done, n - GROUP + 1)
                ac.activation(v1[:, m % GROUP, :].rearrange("p (h e) -> p h e", e=HE)[:, :, 0:HD],
                              qkv_ps[:, 2 * D:3 * D].rearrange("p (h d) -> p h d", d=HD),
                              ACT.Copy).then_inc(act_in, 1)

            def copy_qT(g, m):
                n = GROUP * g + m
                ac.wait_ge(qTp_done, n + 1)
                after(ac, inter_done, n - 1)
                ac.copy(qT[:, m % 2, :], qT_ps).then_inc(qT_done, 1)

            def copy_oT(g, m):
                n = GROUP * g + m
                ac.wait_ge(oTp_done, n + 1)
                after(ac, y_done, n - 1)
                ac.copy(oT[:, m % 2, :], oT_ps).then_inc(oT_done, 1)

            def copy_y(g, m, aside):
                n, s = GROUP * g + m, m % GROUP
                ac.wait_ge(y_done, n + 1)
                after(ac, negm_done, g + m // GROUP)
                ac.activation(y[:, GROUP if aside else s, :], y_ps, ACT.Identity, accum_out=ysum[:, s:s + 1]).then_inc(y_used, 1)

            def spread(g):
                ac.wait_ge(negm_done, g + 1)
                after(ac, y_moved, g)
                for i in range(GROUP):
                    after(ac, ssq_done, GROUP * g + i)
                    ac.activation(junk[:, 0, :], y[:, i, :], ACT.Square, bias=negm[:, i:i + 1],
                                  accum_out=ssq[:, i:i + 1]).then_inc(ssq_done, 1)

            def normalise(g):
                ac.wait_ge(shift_done, g + 1)
                ac.wait_ge(rstd_done, g + 1)
                after(ac, rows_done, GROUP * g)
                ac.wait_ge(z_saved, 16 * (g + 1))
                for i in range(GROUP):
                    ac.activation(zs[:, i, :], y[:, i, :], ACT.Identity, bias=shift[:, i:i + 1],
                                  scale=rstd[:, i:i + 1]).then_inc(z_done, 1)

            def move_y(g):
                ac.wait_ge(z_done, GROUP * g + GROUP)
                ac.wait_ge(y_used, GROUP * g + GROUP + 1)
                ac.copy(y[:, 0, :], y[:, GROUP, :]).then_inc(y_moved, 1)

            def squares(g):
                for i in range(GROUP):
                    ac.wait_ge(z_done, GROUP * g + i + 1)
                    after(ac, zsq_done, GROUP * g + i)
                    ac.activation(junk[:, 1, :], zs[:, i, :], ACT.Square,
                                  accum_out=zsq[:, i:i + 1]).then_inc(zsq_done, 1)

            def copy_zT(g):
                ac.wait_ge(zTp_done, g + 1)
                ac.copy(zT[:, :, :].rearrange("p c t -> p (c t)"), turn_ps[:, :]).then_inc(zT_done, 1)

            def copy_logits(g):
                ac.wait_ge(lg_done, g + 1)
                ac.copy(lgs[:, :, :].rearrange("p c e -> p (c e)"), lg_ps).then_inc(lgs_done, 1)

            def fill_rows(g):
                ac.wait_ge(scattered, 16 * (K * GROUP * g + 1))
                for i in range(GROUP):
                    ac.activation(rows[:, i, :, 0:D], zs[:, i, :].unsqueeze(1).to_broadcast([P, K, D]),
                                  ACT.Copy).then_inc(rows_done, 1)

            def exp_logits(g):
                ac.wait_ge(dlog_done, g + 1)
                ac.activation(R["elog"][:, :, :], R["dlog"][:, :, :], ACT.Exp).then_inc(elog_done, 1)

            ac.wait_ge(pool_set_up, 2)

            def step(g, m, route):
                if exists(g, m + 2):
                    inputs(g, m + 2)
                if exists(g, m - 1):
                    copy_qT(g, m - 1)
                if route == 0:
                    spread(g - 1)
                if exists(g, m - 2):
                    copy_oT(g, m - 2)
                if route == 1:
                    normalise(g - 1)
                    if exists(g, m - 3):
                        move_y(g - 1)
                if route == 1:
                    copy_zT(g - 1)
                if route == 2:
                    copy_logits(g - 1)
                if exists(g, m - 2):
                    copy_y(g, m - 2, route == 0)
                if route == 1:
                    squares(g - 1)
                if route == 2:
                    exp_logits(g - 1)
                if route == 3:
                    fill_rows(g - 1)

            groups(ac, step)
            last = GROUPS - 1
            spread(last)
            normalise(last)
            squares(last)
            copy_zT(last)
            copy_logits(last)
            exp_logits(last)
            fill_rows(last)

            def copy_zinT(k, b, rnd):
                ac.wait_ge(zinTp_done, k + 1)
                after(ac, gate_done, k - 1)
                ac.copy(zinT[:, b % 2, :], zinT_ps[b % 2][:, 0:P]).then_inc(zinT_done, 1)

            def gelu_gate(k, b, rnd):
                ac.wait_ge(gate_done, k + 1)
                after(ac, act_done, k - 1)
                ac.activation(gelu[:, b % 2, :], gate_ps[b % 2][:, 0:HID], ACT.Gelu_apprx_tanh).then_inc(gelu_done, 1)

            def copy_actT(k, b, rnd):
                ac.wait_ge(actTp_done, k + 1)
                after(ac, yp_done, k - 1)
                ac.copy(actT[:, b % 2, :, :].rearrange("p h t -> p (h t)"), actT_ps[b % 2][:, 0:HID])\
                  .then_inc(actT_done, 1)

            tiles(ac, copy_zinT, gelu_gate, copy_actT, None, (0, 1, 2))

            for g in range(GROUPS):
                ac.wait_ge(fneg_done, g + 1)
                for i in range(GROUP * g, GROUP * g + GROUP):
                    if i:
                        ac.wait_ge(fssq_done, i)
                    ac.activation(junk[:, 0, :], s2[:, i, :], ACT.Square, bias=fneg[:, i:i + 1],
                                  accum_out=fssq[:, i:i + 1]).then_inc(fssq_done, 1)

        @block.vector
        def _(ve):
            st = Steps(ve, dve_steps)
            ve.memset(zero[:, :], 0.0).then_inc(set_up, 1)
            ve.wait_ge(c_loaded, 16)
            ve.tensor_copy(tok[:, :], const("tok")).then_inc(set_up, 1)
            ve.wait_ge(wr_loaded, 32)
            ve.wait_ge(scattered, 16)
            ve.wait_ge(z_saved, 16)
            ve.tensor_scalar(w_r[:, :], w_r0[:, :], w_rs[:, 0:1], None, ALU.mult).then_inc(set_up, 1)
            st.chain(ve.tensor_copy(base[:, 0, :], const("ebase")))
            lead = st.n

            def heads(t, n=H):
                return t.rearrange("p (h e) -> p h e", e=HE)

            def features(g, m):
                n, s = GROUP * g + m, m % GROUP
                ve.wait_ge(act_in, 3 * (n + 1))
                after(ve, state_done, n - GROUP + 1)
                after(ve, kv_done, n - GROUP + 1)
                ve.scalar_tensor_tensor(out=qk[:, s, :], in0=eqk[:, m % 2, :], scalar=1.0, in1=rqk[:, m % 2, :],
                                        op0=ALU.min, op1=ALU.add).then_inc(phi_done, 1)

            def mask_state(g, m):
                n = GROUP * g + m
                if isinstance(g, int) and n < 1:
                    ve.wait_ge(state_zero, 1)
                else:
                    ve.wait_ge(state_done, n)
                after(ve, inter_done, n - 1)
                ve.tensor_tensor(state_m[:, m % 2, :], state_ps, const("block"), ALU.mult).then_inc(state_used, 1)

            def attend(g, m, between):
                n, s = GROUP * g + m, m % GROUP
                q = qk[:, s, 0:D].rearrange("p (h d) -> p h d", d=HD)
                for b, (h0, h1) in enumerate(HEADS):
                    ve.wait_ge(pre_done, 3 * n + b + 1)
                    if b == 0:
                        after(ve, summed, n)
                    nh = h1 - h0
                    cols = nh * HE * HD
                    ve.tensor_tensor(
                        prod[:, h0 * HE * HD:h1 * HE * HD].rearrange("p (h e d) -> p h e d", e=HE, d=HD),
                        pre_ps[b][:, 0:cols].rearrange("p (h e d) -> p h e d", e=HE, d=HD),
                        q[:, h0:h1, :].unsqueeze(2).to_broadcast([P, nh, HE, HD]), ALU.mult).then_inc(pre_used, 1)
                    between(b)
                ve.wait_ge(pre_used, 3 * (n + 1))
                after(ve, inter_used, n)
                ve.tensor_reduce(num[:, :], prod[:, :].rearrange("p (c d) -> p c d", d=HD), AX.X,
                                 ALU.add).then_inc(summed, 1)
                between(3)
                if exists(g, m + 1):
                    mask_state(g, m + 1)
                between(4)
                ve.wait_ge(inter_done, n + 1)
                ve.wait_ge(summed, n + 1)
                after(ve, o_done, n)
                ve.tensor_tensor(num2[:, :], inter_ps, num[:, :], ALU.add).then_inc(inter_used, 1)
                if exists(g, m + 3):
                    features(g, m + 3)
                between(5)
                ve.wait_ge(inter_used, n + 1)
                ve.tensor_scalar(den[:, :], heads(num2[:, :])[:, :, HD], DEN_MIN, None, ALU.max).then_inc(den_done, 1)
                between(6)
                ve.wait_ge(den_done, n + 1)
                ve.reciprocal(rden[:, :], den[:, :]).then_inc(rden_done, 1)
                between(7)
                ve.wait_ge(rden_done, n + 1)
                after(ve, oTp_done, n - 1)
                ve.tensor_tensor(o[:, m % 2, :].rearrange("p (h d) -> p h d", d=HD), heads(num2[:, :])[:, :, 0:HD],
                                 rden[:, :].unsqueeze(2).to_broadcast([P, H, HD]), ALU.mult).then_inc(o_done, 1)
                between(8)

            def by_token(t):
                return t.unsqueeze(2).to_broadcast([P, GROUP, E])

            def by_rank(t):
                return t.unsqueeze(1).to_broadcast([P, K, GROUP, E])

            def tt(out, a, b, op, last=0):
                st.ready(last)
                st.did(ve.tensor_tensor(out, a, b, op))

            def ts(out, a, s1, s2, op0, op1=None, last=0):
                st.ready(last)
                st.did(ve.tensor_scalar(out, a, s1, s2, op0) if op1 is None else
                       ve.tensor_scalar(out, a, s1, s2, op0, op1))

            def reduce(out, a, op, last=0):
                st.ready(last)
                st.did(ve.tensor_reduce(out, a, AX.X, op))

            def inverse(out, a, last=0):
                st.ready(last)
                st.did(ve.reciprocal(out, a))

            def copy(out, a, last=0):
                st.ready(last)
                st.did(ve.tensor_copy(out, a))

            desc = const("desc").rearrange("p (c e) -> p c e", e=E)
            A = {n: t[:, :, :] for n, t in R.items()} | {n: t[:, :] for n, t in R1.items()}
            rank_of, tot_of = rank[:, 0], rank[:, 1]

            def mean_and_variance(g, i):
                if i == 0:
                    ve.wait_ge(y_used, GROUP * g + GROUP)
                    ve.tensor_scalar(negm[:, :], ysum[:, :], -1.0 / D, None, ALU.mult).then_inc(negm_done, 1)
                if i == 4:
                    ve.wait_ge(ssq_done, GROUP * g + GROUP)
                    ve.tensor_scalar(vare[:, :], ssq[:, :], 1.0 / D, LN_EPS, ALU.mult, ALU.add)\
                      .then_inc(vare_done, 1)

                if i == 8:
                    ve.wait_ge(rstd_done, g + 1)
                    ve.wait_ge(negm_done, g + 1)
                    ve.tensor_tensor(shift[:, :], negm[:, :], rstd[:, :], ALU.mult).then_inc(shift_done, 1)

            def choose(g, i):
                if i == 0:
                    ve.wait_ge(zsq_done, GROUP * g + GROUP)
                    ve.tensor_scalar(zsqe[:, :], zsq[:, :], D * RMS_EPS, None, ALU.add).then_inc(zsqe_done, 1)
                if i == 3:
                    ve.wait_ge(lgs_done, g + 1)
                    ve.wait_ge(rrms_done, g + 1)
                    tt(A["logit"], lgs[:, :, :], by_token(A_rrms), ALU.mult)
                if i == 4:
                    reduce(A["m1"], A["logit"], ALU.max)
                    tt(A["eq1"], A["logit"], by_token(A["m1"]), ALU.is_equal)
                if i == 5:
                    tt(A["key1"], A["eq1"], desc, ALU.mult)
                    reduce(A["k1"], A["key1"], ALU.max)
                if i == 6:
                    tt(A["ind1"], desc, by_token(A["k1"]), ALU.is_equal)
                    ve.tensor_tensor(A["dlog"], A["logit"], by_token(A["m1"]), ALU.subtract).then_inc(dlog_done, 1)
                    st.ready()
                    st.did(ve.scalar_tensor_tensor(out=A["rest"], in0=A["ind1"], scalar=BELOW, in1=A["logit"],
                                                   op0=ALU.mult, op1=ALU.add))
                if i == 7:
                    reduce(A["m2"], A["rest"], ALU.max)
                    tt(A["eq2"], A["rest"], by_token(A["m2"]), ALU.is_equal)
                if i == 8:
                    tt(A["key2"], A["eq2"], desc, ALU.mult)
                    reduce(A["k2"], A["key2"], ALU.max)
                    tt(A["ind2"], desc, by_token(A["k2"]), ALU.is_equal)
                    st.ready()
                    ve.tensor_tensor(A["ind"], A["ind1"], A["ind2"], ALU.add).then_inc(ind_done, 1)

            def weigh_and_place(g, i):
                if i == 0:
                    ve.wait_ge(elog_done, g + 1)
                    reduce(A["esum"], A["elog"], ALU.add)
                    inverse(A["einv"], A["esum"])
                if i == 1:
                    ve.wait_ge(ind_done, g + 1)
                    tt(A["prob"], A["elog"], by_token(A["einv"]), ALU.mult)
                    tt(A["gw"], A["prob"], A["ind"], ALU.mult)
                if i == 2:
                    reduce(A["ren"], A["gw"], ALU.add)
                    ve.wait_ge(rank_done, 2 * g + 2)
                    ve.tensor_copy(rank[:, :, :, :].rearrange("p k c e -> p (k c e)"), rank_ps)\
                      .then_inc(rank_used, 1)
                if i == 3:
                    st.ready()
                    st.did(ve.scalar_tensor_tensor(out=A["reng"], in0=A["ren"], scalar=0.0, in1=A["ren"],
                                                   op0=ALU.is_le, op1=ALU.add))
                    ve.wait_ge(rank_used, g + 1)
                    tt(base[:, 1, :], tot_of[:, 0, :], base[:, 0, :], ALU.add, last=1)
                if i == 4:
                    inverse(A["renr"], A["reng"], last=1)
                    tt(base[:, 2, :], tot_of[:, 1, :], base[:, 1, :], ALU.add, last=1)
                if i == 5:
                    tt(A["comb"], A["gw"], by_token(A["renr"]), ALU.mult, last=1)
                    tt(base[:, 3, :], tot_of[:, 2, :], base[:, 2, :], ALU.add, last=1)
                if i == 6:
                    tt(A["combs"], A["comb"], pes_b[:, :].unsqueeze(1).to_broadcast([P, GROUP, E]), ALU.mult, last=1)
                    tt(base[:, 4, :], tot_of[:, 3, :], base[:, 3, :], ALU.add, last=1)
                if i == 7:
                    tt(comb12[:, :, :, :], by_rank(A["combs"]), ind12[:, :, :, :], ALU.mult, last=1)
                    tt(A["pos"], rank_of, base[:, 0:GROUP, :], ALU.add, last=1)
                if i == 8:
                    ve.wait_ge(scattered, 16 * (K * GROUP * g + 1))
                    reduce(rows[:, :, :, D].rearrange("p c r -> p r c"), comb12[:, :, :, :], ALU.add, last=1)
                    tt(pos12[:, :, :, :], by_rank(A["pos"]), ind12[:, :, :, :], ALU.mult, last=1)
                    copy(rows[:, :, :, D + 1].bitcast(I32).rearrange("p c r -> p r c"),
                         tok[:, :].rearrange("p (r c) -> p r c", c=GROUP), last=1)
                    reduce(slot_f[:, :].rearrange("p (r c) -> p r c", c=GROUP), pos12[:, :, :, :], ALU.add, last=1)
                    ts(tok[:, :], tok[:, :], float(GROUP * P), None, ALU.add, last=1)
                    copy(slot[:, :], slot_f[:, :], last=1)
                    st.ready()
                    ve.tensor_copy(base[:, 0, :], base[:, GROUP, :]).then_inc(route_done, 1)

            A_rrms = rrms[:, :]
            parts = (mean_and_variance, lambda g, i: None, choose, weigh_and_place)

            def step(g, m, route):
                def between(i):
                    if route is not None:
                        parts[route](g - 1, i)
                if route == 0 and (not isinstance(g, int) or g > 1):
                    ve.wait_ge(route_done, g - 1)
                if exists(g, m - 1):
                    attend(g, m - 1, between)
                else:
                    if exists(g, m + 2):
                        features(g, m + 2)
                    if isinstance(g, int) and g == 0 and m == 0:
                        mask_state(0, 0)
                    for i in range(9):
                        between(i)

            ROUTE_STEPS = 12 + 21
            groups(ve, step, lambda g: st.start(lead + ROUTE_STEPS * (g - 1)))
            assert st.n == ROUTE_STEPS, st.n
            last = GROUPS - 1
            st.start(lead + ROUTE_STEPS * last)
            ve.wait_ge(route_done, last)
            for part in parts:
                for i in range(9):
                    part(last, i)
            ve.wait_ge(route_done, GROUPS)
            assert st.n == ROUTE_STEPS, st.n

            ve.tensor_copy(cnt_i[:, :], base[:, 0, :]).then_inc(cnt_done, 1)
            st.chain(ve.scalar_tensor_tensor(out=nt_f[:, :], in0=base[:, 0, :], scalar=float(P - 1),
                                             in1=const("ebase"), op0=ALU.add, op1=ALU.subtract))
            st.chain(ve.tensor_copy(nt_i[:, :], nt_f[:, :]))
            st.chain(ve.tensor_scalar(nt_s[:, :], nt_i[:, :], P.bit_length() - 1, None, ALU.arith_shift_right))
            st.chain(ve.tensor_copy(ntile[:, :], nt_s[:, :]))
            cum = ntile
            for by, nxt in ((1, cumA), (2, cumB), (4, cumC)):
                st.did(ve.tensor_copy(nxt[:, 0:by], cum[:, 0:by]))
                st.chain(ve.tensor_tensor(nxt[:, by:E], cum[:, by:E], cum[:, 0:E - by], ALU.add))
                cum = nxt
            st.chain(ve.tensor_scalar(skip[:, :], ntile[:, :], float(-P), float(REGION), ALU.mult, ALU.add))
            a, b = CONST["tile"]
            num_t = C[0:1, a:b]
            tt(past[:, :, :], cum[0:1, :].unsqueeze(1).to_broadcast([1, TILES, E]),
               num_t.unsqueeze(2).to_broadcast([1, TILES, E]), ALU.is_le)
            st.ready()
            tt(pskip[:, :, :], past[:, :, :], skip[0:1, :].unsqueeze(1).to_broadcast([1, TILES, E]), ALU.mult)
            st.ready()
            st.chain(ve.tensor_reduce(te_f[:, :], past[:, :, :], AX.X, ALU.add))
            st.chain(ve.tensor_reduce(tr_f[:, :], pskip[:, :, :], AX.X, ALU.add))
            st.chain(ve.tensor_scalar(te_g[:, :], te_f[:, :], float(E - 1), float(EW), ALU.min, ALU.mult))
            st.chain(ve.tensor_copy(tile_w[:, :], te_g[:, :]))
            st.chain(ve.scalar_tensor_tensor(out=tr_g[:, :], in0=num_t, scalar=float(P), in1=tr_f[:, :],
                                             op0=ALU.mult, op1=ALU.add))
            ve.tensor_copy(tile_r[:, :], tr_g[:, :]).then_inc(table_done, 1)
            ve.wait_ge(table_done, 1)

            def activate(k, b, rnd):
                ve.wait_ge(gelu_done, k + 1)
                ve.wait_ge(gate_done, k + 1)
                ve.wait_ge(zin_loaded[b], 16 * (rnd + 1))
                after(ve, actTp_done, k - 1)
                ve.scalar_tensor_tensor(out=act[:, b % 2, :], in0=gelu[:, b % 2, :], scalar=zin[:, b, D:D + 1],
                                        in1=gate_ps[b % 2][:, HID:2 * HID], op0=ALU.mult, op1=ALU.mult)\
                  .then_inc(act_done, 1)

            def take(k, b, rnd):
                ve.wait_ge(yp_done, k + 1)
                ve.tensor_copy(yout[:, b, :], yout_ps[b % 2][:, 0:D]).then_inc(yout_done, 1)

            tiles(ve, None, activate, None, take, (1, 3))

            ve.wait_ge(z_saved, 16 * (GROUPS + 1))

            def total(g):
                c = slice(GROUP * g, GROUP * g + GROUP)
                ve.wait_ge(pl_loaded[g], 32)
                st.chain(ve.tensor_tensor(s1[:, c, :], pl[:, 0, c, :], pl[:, 1, c, :], ALU.add))
                for i in range(GROUP * g, GROUP * g + GROUP):
                    ve.scalar_tensor_tensor(out=s2[:, i, :], in0=s1[:, i, :], scalar=1.0, in1=zall[:, i, :],
                                            op0=ALU.mult, op1=ALU.add,
                                            accum_out=fsum[:, i:i + 1]).then_inc(fsum_done, 1)
                ve.wait_ge(fsum_done, GROUP * (g + 1))
                ve.tensor_scalar(fneg[:, c], fsum[:, c], -1.0 / D, None, ALU.mult).then_inc(fneg_done, 1)

            def scale(g):
                c = slice(GROUP * g, GROUP * g + GROUP)
                ve.wait_ge(fssq_done, GROUP * (g + 1))
                ve.tensor_scalar(fvar[:, c], fssq[:, c], 1.0 / D, LN_EPS, ALU.mult, ALU.add).then_inc(fvar_done, 1)

            def finish(g):
                ve.wait_ge(frs_done, g + 1)
                for i in range(GROUP * g, GROUP * g + GROUP):
                    ve.tensor_scalar(res[:, i, :], s2[:, i, :], fneg[:, i:i + 1], frs[:, i:i + 1], ALU.add,
                                     ALU.mult).then_inc(res_done, 1)

            total(0)
            for g in range(1, GROUPS):
                total(g)
                scale(g - 1)
                if g >= 2:
                    finish(g - 2)
            ve.wait_ge(fneg_done, GROUPS)
            scale(GROUPS - 1)
            finish(GROUPS - 2)
            finish(GROUPS - 1)


def constants():
    import numpy as np

    c = np.zeros((P, NCONST), np.float32)
    i = np.arange(P)

    def put(name, v):
        a, b = CONST[name]
        c[:, a:b] = v

    put("tri", i[:, None] <= i[None, :])
    put("stri", i[:, None] < i[None, :])
    put("ident", np.eye(P))
    put("ones", 1.0)
    put("block", (i[:, None] // HD) == (np.arange(H * HE)[None, :] // HE))
    put("desc", np.tile(E - np.arange(E), GROUP)[None, :])
    put("tok", i[:, None] + (T * np.arange(K)[:, None] + P * np.arange(GROUP)[None, :]).reshape(1, -1))
    put("ebase", (np.arange(E) * REGION)[None, :])
    put("tile", np.arange(TILES)[None, :])
    put("half", -0.5)
    put("pad", K * T + i[:, None] + P * np.arange(PADS)[None, :])
    return c


def kernel(**inputs):
    import numpy as np
    import concourse.bacc as bacc
    from concourse.bass_utils import run_bass_kernel_spmd

    a = {k: np.asarray(v) for k, v in inputs.items()}
    x = a["L0_attn_x"].reshape(T, D)
    wqkv = np.concatenate([a["L0_attn_Wq"].T, a["L0_attn_Wk"].T, a["L0_attn_Wv"].T], axis=1)
    arrays = {
        "xT": x.T,
        "x": x,
        "wqkv": wqkv,
        "wo": a["L0_attn_Wo"].T,
        "rw": a["L0_ffn_router_w"],
        "rscale": a["L0_ffn_router_scale"].reshape(D, 1),
        "pes": np.broadcast_to(a["L0_ffn_per_expert_scale"].reshape(1, E), (P, E)),
        "expert_w": np.concatenate(
            [a["L0_ffn_gating_w"].transpose(3, 0, 1, 2).reshape(D, E, 2 * HID),
             a["L0_ffn_linear_w"].reshape(E, HB, P, D).transpose(2, 0, 1, 3).reshape(P, E, HB * D)],
            axis=2).reshape(D, E * EW),
        "consts": constants(),
    }
    arrays = {k: np.ascontiguousarray(v) for k, v in arrays.items()}
    nc = bacc.Bacc("TRN2", target_bir_lowering=False, num_devices=1)
    args = [nc.dram_tensor("in_" + k, v.shape, F32, kind="ExternalInput").ap() for k, v in arrays.items()]
    out = nc.dram_tensor("out_0", (T, D), F32, kind="ExternalOutput").ap()
    build(nc, *args, out)
    r = run_bass_kernel_spmd(nc, [{"in_" + k: v for k, v in arrays.items()}], core_ids=[0])
    return r.results[0]["out_0"].reshape(1, T, D)
```

```python
from contextlib import ExitStack

import concourse.bass as bass
from concourse import mybir
from concourse.alu_op_type import AluOpType as ALU

F32 = mybir.dt.float32
F32R = mybir.dt.float32r
I32 = mybir.dt.int32
U32 = mybir.dt.uint32
ACT = mybir.ActivationFunctionType
AX = mybir.AxisListType

P = 128
D = 128
T = 2048
CHUNKS = T // P
GROUP = 4
GROUPS = CHUNKS // GROUP
PAIR = 2
PAIRS = CHUNKS // PAIR
PE_PAIRS = (3, 5, 6, 7)
POOL_PAIRS = (1, 2, 4)
V_PAIR = PAIRS - 1
H, HD = 16, 8
HE = HD + 1
KV = H * HE * HD
HEADS = [(0, 6), (6, 12), (12, 16)]
E, K, HID = 8, 2, 256
HB = HID // P
REGION = T + P
SPARE = E * REGION
BUFS = 8
FULL = T * K // P
TILES = FULL + E - 1
ROUNDS, REST = divmod(TILES, BUFS)
NSPARE = TILES - FULL
PADS = E + NSPARE
ROW = D + 2
LN_EPS, RMS_EPS, DEN_MIN = 1e-5, 1e-6, 1e-6
BELOW = -3.0e38

CONST = {}
_at = 0
for _name, _n in (("tri", P), ("stri", P), ("ident", P), ("ones", P), ("block", H * HE), ("desc", GROUP * E),
                  ("tok", K * GROUP), ("ebase", E), ("tile", TILES), ("half", GROUP), ("pad", PADS)):
    CONST[_name] = (_at, _at + _n)
    _at += _n
NCONST = _at


class Steps:

    def __init__(self, eng, sem):
        self.eng, self.sem, self.base, self.n = eng, sem, 0, 0

    def start(self, base):
        self.base, self.n = base, 0

    def ready(self, last=0):
        self.eng.wait_ge(self.sem, self.base + self.n - last)

    def did(self, ins):
        ins.then_inc(self.sem, 1)
        self.n += 1

    def chain(self, ins):
        self.did(ins)
        self.ready()


def build(nc, xT, x, wqkv, wo, rw, rscale, pes, gate_w, lin_w, consts, out):
    zbuf = nc.dram_tensor("zbuf", (SPARE + NSPARE * P, ROW), F32, kind="Internal").ap()
    both = nc.dram_tensor("both", (K * T + PADS * P, D), F32, kind="Internal").ap()

    with ExitStack() as ctx:
        def sb(name, shape, dt=F32):
            return ctx.enter_context(nc.sbuf_tensor(name, shape, dt))

        def bank(name, shape):
            return ctx.enter_context(nc.psum_tensor(name, shape, F32))

        def sem(name):
            return ctx.enter_context(nc.semaphore(name))

        C = sb("C", [P, NCONST])

        def const(name):
            a, b = CONST[name]
            return C[:, a:b]

        w_qkv = sb("w_qkv", [P, 3 * D])
        w_o = sb("w_o", [P, D])
        w_r0 = sb("w_r0", [P, E])
        w_rs = sb("w_rs", [P, 1])
        w_r = sb("w_r", [P, E])
        pes_b = sb("pes_b", [P, E])
        w_g = sb("w_g", [P, E, 2 * HID])
        w_l = sb("w_l", [P, E * HB * D])
        w_hi = sb("w_hi", [P, E, 2 * HID], F32R)
        w_lo = sb("w_lo", [P, E, 2 * HID], F32R)
        xTs = sb("xTs", [P, GROUP, P])
        xs = sb("xs", [P, CHUNKS, D])
        eqk = sb("eqk", [P, 2, 2 * D])
        rqk = sb("rqk", [P, 2, 2 * D])
        qk = sb("qk", [P, GROUP, 2 * D])
        v1 = sb("v1", [P, GROUP, H * HE])
        kv = sb("kv", [P, GROUP, KV])
        prod = sb("prod", [P, KV])
        num = sb("num", [P, H * HE])
        num2 = sb("num2", [P, H * HE])
        den = sb("den", [P, H])
        rden = sb("rden", [P, H])
        o = sb("o", [P, 2, D])
        qT = sb("qT", [P, 2, P])
        oT = sb("oT", [P, 2, P])
        state_m = sb("state_m", [P, 2, H * HE])
        pads = sb("pads", [P, PADS, ROW])
        zero = sb("zero", [P, H * HE])
        y = sb("y", [P, GROUP + 1, D])
        zs = sb("zs", [P, GROUP, D])
        junk = sb("junk", [P, 2, D])
        rows = sb("rows", [P, GROUP, K, ROW])
        rows2 = sb("rows2", [P, GROUP, K, ROW])
        zT = sb("zT", [P, GROUP, P])
        lgs = sb("lgs", [P, GROUP, E])
        ysum = sb("ysum", [P, GROUP])
        negm = sb("negm", [P, GROUP])
        ssq = sb("ssq", [P, GROUP])
        vare = sb("vare", [P, GROUP])
        rstd = sb("rstd", [P, GROUP])
        shift = sb("shift", [P, GROUP])
        zsq = sb("zsq", [P, GROUP])
        zsqe = sb("zsqe", [P, GROUP])
        rrms = sb("rrms", [P, GROUP])
        names = ["logit", "eq1", "key1", "rest", "eq2", "key2", "dlog", "elog", "prob", "ind", "gw", "comb", "combs",
                 "pos"]
        R = {n: sb("r_" + n, [P, GROUP, E]) for n in names}
        names1 = ["m1", "k1", "m2", "k2", "esum", "einv", "ren", "reng", "renr"]
        R1 = {n: sb("r_" + n, [P, GROUP]) for n in names1}
        ind12 = sb("ind12", [P, K, GROUP, E])
        R["ind1"], R["ind2"] = ind12[:, 0], ind12[:, 1]
        comb12 = sb("comb12", [P, K, GROUP, E])
        tok = sb("tok", [P, K * GROUP])
        rank = sb("rank", [P, 2, GROUP, E])
        base = sb("base", [P, GROUP + 1, E])
        pos12 = sb("pos12", [P, K, GROUP, E])
        slot_f = sb("slot_f", [P, K * GROUP])
        slot = sb("slot", [P, K * GROUP], I32)
        slot2 = sb("slot2", [P, K * GROUP], I32)
        cnt_i = sb("cnt_i", [P, E], I32)
        nt_f = sb("nt_f", [P, E])
        nt_i = sb("nt_i", [P, E], I32)
        nt_s = sb("nt_s", [P, E], I32)
        ntile = sb("ntile", [P, E])
        cumA = sb("cumA", [P, E])
        cumB = sb("cumB", [P, E])
        cumC = sb("cumC", [P, E])
        skip = sb("skip", [P, E])
        past = sb("past", [1, TILES, E])
        pskip = sb("pskip", [1, TILES, E])
        te_f = sb("te_f", [1, TILES])
        tr_f = sb("tr_f", [1, TILES])
        tr_g = sb("tr_g", [1, TILES])
        te_g = sb("te_g", [1, TILES])
        tile_e = sb("tile_e", [1, TILES], I32)
        tile_r = sb("tile_r", [1, TILES], I32)
        zin = sb("zin", [P, BUFS, ROW])
        zin_hi = sb("zin_hi", [P, 2, P], F32R)
        zin_lo = sb("zin_lo", [P, 2, P], F32R)
        gelu = sb("gelu", [P, 2, HID])
        act = sb("act", [P, 2, HID])
        actT = sb("actT", [P, 2, HB, P])
        yout = sb("yout", [P, BUFS, D])
        zall = sb("zall", [P, CHUNKS, D])
        pl = sb("pl", [P, CHUNKS, K, D])
        s1, s2, res = pl[:, :, 0], pl[:, :, 1], pl[:, :, 0]
        fstat = sb("fstat", [P, CHUNKS, 6])
        fmv = sb("fmv", [P, CHUNKS, 2])
        fvar = sb("fvar", [P, CHUNKS])
        frs = sb("frs", [P, CHUNKS])
        fshift = sb("fshift", [P, CHUNKS])

        B = [bank(f"bank{i}", [P, 512]) for i in range(8)]
        qkv_ps = B[0]
        pre_ps = B[2:5]
        state_ps = B[5][:, 0:H * HE]
        turn_ps = B[1]
        qT_ps, oT_ps = B[1][:, 0:P], B[1][:, P:2 * P]
        inter_ps, rank_ps = B[6][:, 0:H * HE], B[6][:, 256:256 + 2 * GROUP * E]
        y_ps, lg_ps = B[7][:, 0:D], B[7][:, 256:256 + GROUP * E]
        sum_ps = {g: B[i][:, 0:PAIR * D] for i, g in enumerate(PE_PAIRS)}
        gate_ps, zinT_ps, actT_ps, yout_ps = B[0:2], B[2:4], B[4:6], B[6:8]

        w_loaded = sem("w_loaded")
        c_loaded = sem("c_loaded")
        wr_loaded = sem("wr_loaded")
        wg_loaded = [sem(f"wg_loaded{i}") for i in range(GROUP)]
        wl_loaded = sem("wl_loaded")
        xT_loaded = [sem(f"xT_loaded{j}") for j in range(GROUP)]
        x_loaded = sem("x_loaded")
        set_up = sem("set_up")
        pool_set_up = sem("pool_set_up")
        state_zero = sem("state_zero")
        qkv_done = sem("qkv_done")
        act_in = sem("act_in")
        phi_done = sem("phi_done")
        kv_done = sem("kv_done")
        qTp_done = sem("qTp_done")
        qT_done = sem("qT_done")
        pre_done = sem("pre_done")
        pre_used = sem("pre_used")
        state_used = sem("state_used")
        inter_done = sem("inter_done")
        state_done = sem("state_done")
        inter_used = sem("inter_used")
        o_done = sem("o_done")
        oTp_done = sem("oTp_done")
        oT_done = sem("oT_done")
        y_done = sem("y_done")
        summed = sem("summed")
        den_done = sem("den_done")
        rden_done = sem("rden_done")
        y_used = sem("y_used")
        negm_done = sem("negm_done")
        ssq_done = sem("ssq_done")
        vare_done = sem("vare_done")
        rstd_done = sem("rstd_done")
        shift_done = sem("shift_done")
        z_done = sem("z_done")
        v_z_done = sem("v_z_done")
        zsq_done = sem("zsq_done")
        v_zsq_done = sem("v_zsq_done")
        zTp_done = sem("zTp_done")
        zT_done = sem("zT_done")
        lg_done = sem("lg_done")
        lgs_done = sem("lgs_done")
        zsqe_done = sem("zsqe_done")
        rrms_done = sem("rrms_done")
        dlog_done = sem("dlog_done")
        elog_done = sem("elog_done")
        ind_done = sem("ind_done")
        rank_done = sem("rank_done")
        rank_used = sem("rank_used")
        y_moved = sem("y_moved")
        rows_done = sem("rows_done")
        route_done = sem("route_done")
        scattered = sem("scattered")
        scattered2 = sem("scattered2")
        z_saved = sem("z_saved")
        cnt_done = sem("cnt_done")
        table_done = sem("table_done")
        padded = sem("padded")
        zin_loaded = [sem(f"zin_loaded{j}") for j in range(BUFS)]
        zinTp_done = sem("zinTp_done")
        w_hi_done = sem("w_hi_done")
        w_lo_done = sem("w_lo_done")
        zin_hi_done = sem("zin_hi_done")
        zin_lo_done = sem("zin_lo_done")
        gate_done = sem("gate_done")
        gelu_done = sem("gelu_done")
        act_done = sem("act_done")
        actTp_done = sem("actTp_done")
        actT_done = sem("actT_done")
        yp_done = sem("yp_done")
        yout_done = sem("yout_done")
        placed = [sem(f"placed{j}") for j in range(BUFS)]
        pl_loaded = [sem(f"pl_loaded{g}") for g in range(PAIRS)]
        s1_done = sem("s1_done")
        s1v_done = sem("s1v_done")
        s2_done = sem("s2_done")
        sum_done = sem("sum_done")
        fstat_done = sem("fstat_done")
        fmv_done = sem("fmv_done")
        fvar_done = sem("fvar_done")
        frs_done = sem("frs_done")
        fshift_done = sem("fshift_done")
        res_done = sem("res_done")
        res_v_done = sem("res_v_done")
        stored = sem("stored")
        pads_done = sem("pads_done")
        scatter_go = sem("scatter_go")
        dve_steps = sem("dve_steps")

        def is_last(g):
            return isinstance(g, int) and g == GROUPS - 1

        def has_own(g):
            return isinstance(g, int) and g == GROUPS - 2

        def rows_of(g):
            return rows2 if has_own(g) else rows

        def slot_of(g):
            return slot2 if has_own(g) else slot

        def wait_for_rows(eng, g):
            if not has_own(g):
                eng.wait_ge(scattered, 16 * (K * GROUP * (g - 1 if is_last(g) else g) + 1))

        def total_of(g):
            c = slice(PAIR * g, PAIR * g + PAIR)
            return sum_ps[g].rearrange("p (c d) -> p c d", d=D) if g in PE_PAIRS else s2[:, c, :]

        def exists(g, m):
            return not isinstance(g, int) or 0 <= GROUP * g + m < CHUNKS

        def groups(eng, step, start=lambda g: None):
            for m in range(-2, 2):
                step(0, m, None)
            for m in range(2, 6):
                step(0, m, None)
            with eng.Fori(1, GROUPS - 1) as g:
                start(g)
                for m in range(2, 6):
                    step(g, m, m - 2)
            start(GROUPS - 1)
            for m in range(2, 6):
                step(GROUPS - 1, m, m - 2)

        def at(k):
            return slice(k, k + 1) if isinstance(k, int) else bass.ds(k, 1)

        def after(eng, signal, count):
            if not (isinstance(count, int) and count <= 0):
                eng.wait_ge(signal, count)

        def tiles(eng, *stages):
            def step(k, n, rounds=0):
                for lag, stage in stages:
                    if not isinstance(k, int) or 0 <= k - lag < TILES:
                        stage(k - lag, (n - lag) % BUFS, rounds + (n - lag) // BUFS)

            for k in range(REST):
                step(k, k)
            with eng.Fori(0, ROUNDS) as i:
                for b in range(BUFS):
                    step(BUFS * i + (REST + b), REST + b, i)
            for k in range(TILES, TILES + max(lag for lag, _ in stages)):
                step(k, k)

        block = ctx.enter_context(nc.Block())

        @block.sync
        def _(sp):
            sp.dma_start(w_qkv[:, :], wqkv).then_inc(w_loaded, 16)
            for j in range(GROUP):
                sp.dma_start(xTs[:, j, :], xT[:, j * P:(j + 1) * P]).then_inc(xT_loaded[j], 16)
                if j == 0:
                    sp.dma_start(C[:, :], consts).then_inc(c_loaded, 16)
            sp.dma_start(w_o[:, :], wo).then_inc(wr_loaded, 16)
            sp.dma_start(w_rs[:, :], rscale).then_inc(z_saved, 16)
            sp.dma_start(pes_b[:, :], pes).then_inc(wr_loaded, 16)
            sp.dma_start(xs[:, :, :], x.rearrange("(c p) d -> p c d", p=P)).then_inc(x_loaded, 16)

            def save_z(g):
                if is_last(g):
                    sp.wait_ge(z_done, GROUP * g + GROUP // 2)
                    sp.wait_ge(v_z_done, GROUP // 2)
                else:
                    sp.wait_ge(z_done, GROUP * g + GROUP)
                sp.dma_start(zall[:, bass.ds(GROUP * g, GROUP), :], zs[:, :, :]).then_inc(z_saved, 16)

            def load(g):
                for j in range(GROUP):
                    n = GROUP * g + j
                    sp.wait_ge(qkv_done, n - GROUP + 1)
                    sp.dma_start(xTs[:, j, :], xT[:, bass.ds(n * P, P)]).then_inc(xT_loaded[j], 16)
                if not isinstance(g, int):
                    save_z(g - 2)

            load(1)
            for i in range(GROUP):
                e = slice(i * E // GROUP, (i + 1) * E // GROUP)
                sp.dma_start(w_g[:, e, :], gate_w.rearrange("p (e h) -> p e h", e=E)[:, e, :])\
                  .then_inc(wg_loaded[i], 16)
            sp.dma_start(w_l[:, :], lin_w).then_inc(wl_loaded, 16)
            with sp.Fori(2, GROUPS) as g:
                load(g)
            save_z(GROUPS - 2)
            save_z(GROUPS - 1)

            sp.wait_ge(cnt_done, 1)
            sp.wait_ge(pads_done, 1)
            end = sp.alloc_register("rows_end")
            for e in range(E):
                sp.reg_load(end, cnt_i[0:1, e:e + 1])
                at = sp.snap(end, min_val=0, max_val=SPARE - P)
                sp.dma_start(zbuf[bass.ds(at, P), :], pads[:, e, :]).then_inc(padded, 16)
            sp.dma_start(zbuf[SPARE:, :].rearrange("(b p) r -> p b r", p=P), pads[:, E:, :]).then_inc(padded, 16)
            sp.wait_ge(table_done, 1)
            first_rows = []
            for b in range(BUFS):
                row = sp.alloc_register(f"tile_row{b}")
                sp.reg_load(row, tile_r[0:1, b:b + 1])
                first_rows.append(sp.snap(row, min_val=0, max_val=SPARE + (NSPARE - 1) * P))
            sp.wait_ge(padded, 16 * (E + 1))
            sp.wait_ge(scattered, 16 * (K * (CHUNKS - GROUP) + 1))
            sp.wait_ge(scattered2, 16 * K * GROUP)
            for b in range(BUFS):
                sp.dma_start(zin[:, b, :], zbuf[bass.ds(first_rows[b], P), :]).then_inc(zin_loaded[b], 16)
            with sp.Fori(1, ROUNDS) as i:
                for b in range(BUFS):
                    k = BUFS * i + b
                    sp.reg_load(row, tile_r[0:1, bass.ds(k, 1)])
                    at = sp.snap(row, min_val=0, max_val=SPARE + (NSPARE - 1) * P)
                    sp.wait_ge(placed[b], 16 * i)
                    sp.dma_start(zin[:, b, :], zbuf[bass.ds(at, P), :]).then_inc(zin_loaded[b], 16)
            for k in range(BUFS * ROUNDS, TILES):
                b = k % BUFS
                sp.reg_load(row, tile_r[0:1, k:k + 1])
                at_row = sp.snap(row, min_val=0, max_val=SPARE + (NSPARE - 1) * P)
                sp.wait_ge(placed[b], 16 * ROUNDS)
                sp.dma_start(zin[:, b, :], zbuf[bass.ds(at_row, P), :]).then_inc(zin_loaded[b], 16)
            for b in range(BUFS):
                sp.wait_ge(placed[b], 16 * (ROUNDS + (b < REST)))
            for g in range(PAIRS):
                a = K * g * PAIR * P
                sp.dma_start(pl[:, g * PAIR:(g + 1) * PAIR, :, :].rearrange("p c k d -> p c (k d)"),
                             both[a:a + K * PAIR * P, :].rearrange("(c p k) d -> p c (k d)", p=P, k=K))\
                  .then_inc(pl_loaded[g], 16)
            for g in range(PAIRS):
                if g == V_PAIR:
                    sp.wait_ge(res_v_done, PAIR)
                else:
                    sp.wait_ge(res_done, PAIR * (g + 1))
                sp.dma_start(out[g * PAIR * P:(g + 1) * PAIR * P, :].rearrange("(c p) d -> p c d", p=P),
                             res[:, g * PAIR:(g + 1) * PAIR, :]).then_inc(stored, 16)
            sp.wait_ge(stored, 16 * PAIRS)

        @block.gpsimd
        def _(pool):
            pool.dma_start(w_r0[:, :], rw).then_inc(scattered, 16)
            pool.memset(v1[:, :, :], 1.0).then_inc(pool_set_up, 1)
            pool.memset(pads[:, :, :], 0.0).then_inc(pool_set_up, 1)
            pool.wait_ge(c_loaded, 16)
            pool.wait_ge(pool_set_up, 2)
            pool.tensor_copy(pads[:, :, D + 1].bitcast(I32), const("pad"))\
                .then_inc(pads_done, 1)

            def outer(g, m):
                n, s = GROUP * g + m, m % GROUP
                pool.wait_ge(phi_done, n + 1)
                after(pool, pre_done, 3 * (n - GROUP + 1))
                a = v1[:, s, :].rearrange("p (h e) -> p h e", e=HE).unsqueeze(3).to_broadcast([P, H, HE, HD])
                b = qk[:, s, D:2 * D].rearrange("p (h d) -> p h d", d=HD).unsqueeze(2).to_broadcast([P, H, HE, HD])
                pool.tensor_tensor(kv[:, s, :].rearrange("p (h e d) -> p h e d", e=HE, d=HD), a, b,
                                   ALU.mult).then_inc(kv_done, 1)

            def norm_pow(g):
                pool.wait_ge(vare_done, g + 1)
                pool.tensor_tensor(rstd[:, :], vare[:, :], const("half"), ALU.pow).then_inc(rstd_done, 1)

            def rms_pow(g):
                pool.wait_ge(zsqe_done, g + 1)
                pool.tensor_tensor(rrms[:, :], zsqe[:, :], const("half"), ALU.pow).then_inc(rrms_done, 1)

            def scatter(g, part=range(GROUP), of_rank=range(K)):
                pool.wait_ge(route_done, g + 1)
                for j in part:
                    pool.wait_ge(rows_done, GROUP * g + j + 1)
                    for r in of_rank:
                        c = r * GROUP + j
                        pool.indirect_dma_start(
                            zbuf, bass.IndirectOffsetOnAxis(ap=slot_of(g)[:, c:c + 1].bitcast(U32), axis=0),
                            rows_of(g)[:, j, r, :], None)\
                            .then_inc(scattered2 if has_own(g) else scattered, 16)

            def step(g, m, route):
                if route == 0:
                    if g >= 2:
                        scatter(g - 2, (0,))
                    norm_pow(g - 1)
                if route == 2:
                    rms_pow(g - 1)
                if exists(g, m + 2):
                    outer(g, m + 2)
                if route == 0 and g >= 2:
                    scatter(g - 2, (1,))
                if route == 2 and g >= 2:
                    scatter(g - 2, (2, 3))

            for m in range(-2, 2):
                step(0, m, None)
            for g in range(GROUPS):
                for m in range(2, 6):
                    step(g, m, m - 2 if g else None)
            last = GROUPS - 1
            norm_pow(last)
            scatter(last - 1, (0,), (0,))
            rms_pow(last)
            scatter(last - 1, (0,), (1,))
            scatter(last - 1, (1, 2, 3))
            scatter(last)

            def place(k, b):
                pool.wait_ge(yout_done, k + 1)
                pool.sem_inc(scatter_go, 1)
                pool.indirect_dma_start(
                    both, bass.IndirectOffsetOnAxis(ap=zin[:, b, D + 1:D + 2].bitcast(U32), axis=0),
                    yout[:, b, :], None).then_inc(placed[b], 16)

            with pool.Fori(0, ROUNDS) as i:
                for b in range(BUFS):
                    place(BUFS * i + b, b)
            for k in range(BUFS * ROUNDS, TILES):
                place(k, k % BUFS)

            def power(g):
                c = slice(PAIR * g, PAIR * g + PAIR)
                pool.wait_ge(fvar_done, g + 1)
                pool.tensor_tensor(frs[:, c], fvar[:, c], const("half")[:, 0:PAIR], ALU.pow).then_inc(frs_done, 1)

            def add(g):
                c = slice(PAIR * g, PAIR * g + PAIR)
                pool.wait_ge(pl_loaded[g], 16)
                pool.tensor_tensor(s1[:, c, :], pl[:, c, 0, :], pl[:, c, 1, :], ALU.add).then_inc(s1_done, 1)

            for g in range(PAIRS + 2):
                if g in POOL_PAIRS:
                    add(g)
                if g >= 2:
                    power(g - 2)

        @block.tensor
        def _(pe):
            def project(g, m):
                n = GROUP * g + m
                pe.wait_ge(xT_loaded[m % GROUP], 16 * (g + m // GROUP + 1))
                after(pe, act_in, 3 * n)
                pe.matmul(qkv_ps[:, 0:3 * D], xTs[:, m % GROUP, :], w_qkv[:, :], start=True, stop=True)\
                  .then_inc(qkv_done, 1)

            def prefix(g, m):
                n, s = GROUP * g + m, m % GROUP
                pe.wait_ge(phi_done, n + 1)
                after(pe, oT_done, n - 1)
                pe.transpose(qT_ps, qk[:, s, 0:D], const("ident")).then_inc(qTp_done, 1)
                pe.wait_ge(kv_done, n + 1)
                for b, (h0, h1) in enumerate(HEADS):
                    after(pe, pre_used, 3 * (n - 1) + b + 1 if not isinstance(g, int) or n else 0)
                    c0, c1 = h0 * HE * HD, h1 * HE * HD
                    pe.matmul(pre_ps[b][:, 0:c1 - c0], const("tri"), kv[:, s, c0:c1], start=True, stop=True)\
                      .then_inc(pre_done, 1)

            def state(g, m):
                n, s = GROUP * g + m, m % GROUP
                pe.wait_ge(state_used, n + 1)
                pe.matmul(state_ps, qk[:, s, D:2 * D], v1[:, s, :], start=False, stop=False,
                          skip_group_check=True).then_inc(state_done, 1)
                pe.wait_ge(qT_done, n + 1)
                after(pe, inter_used, n)
                pe.matmul(inter_ps, qT[:, m % 2, :], state_m[:, m % 2, :], start=True, stop=True)\
                  .then_inc(inter_done, 1)

            def turn_o(g, m):
                n = GROUP * g + m
                pe.wait_ge(o_done, n + 1)
                pe.wait_ge(qT_done, n + 2 if exists(g, m + 1) else CHUNKS)
                pe.transpose(oT_ps, o[:, m % 2, :], const("ident")).then_inc(oTp_done, 1)

            def put_out(g, m):
                n = GROUP * g + m
                after(pe, y_used, n)
                pe.matmul(y_ps, const("ident"), xs[:, at(n), :].rearrange("p c d -> p (c d)"),
                          start=True, stop=False)
                pe.wait_ge(oT_done, n + 1)
                pe.matmul(y_ps, oT[:, m % 2, :], w_o[:, :], start=False, stop=True).then_inc(y_done, 1)

            def turn_z(g):
                pe.wait_ge(z_done, GROUP * g + GROUP)
                for i in range(GROUP):
                    t = pe.transpose(turn_ps[:, i * P:(i + 1) * P], zs[:, i, :], const("ident"))
                t.then_inc(zTp_done, 1)

            def logits(g):
                pe.wait_ge(zT_done, g + 1)
                for i in range(GROUP):
                    t = pe.matmul(lg_ps[:, E * i:E * i + E], zT[:, i, :], w_r[:, :], start=True, stop=True)
                t.then_inc(lg_done, 1)

            def turn_last_z():
                pe.wait_ge(z_done, CHUNKS - GROUP // 2)
                for i in range(GROUP // 2):
                    t = pe.transpose(turn_ps[:, i * P:(i + 1) * P], zs[:, i, :], const("ident"))
                t.then_inc(zTp_done, 1)
                pe.wait_ge(v_z_done, GROUP // 2)
                pe.wait_ge(act_in, 3 * CHUNKS)
                for i in range(GROUP // 2, GROUP):
                    t = pe.transpose(qkv_ps[:, i * P:(i + 1) * P], zs[:, i, :], const("ident"))
                t.then_inc(zTp_done, 1)

            def last_logits():
                for i in range(GROUP):
                    if i % (GROUP // 2) == 0:
                        pe.wait_ge(zT_done, GROUPS + i // (GROUP // 2))
                    t = pe.matmul(lg_ps[:, E * i:E * i + E], zT[:, i, :], w_r[:, :], start=True, stop=True)
                t.then_inc(lg_done, 1)

            def ranks(g):
                pe.wait_ge(ind_done, g + 1)
                flat = R["ind"][:, :, :].rearrange("p c e -> p (c e)")
                n = GROUP * E
                pe.matmul(rank_ps[:, 0:n], const("stri"), flat, start=True, stop=True).then_inc(rank_done, 1)
                pe.matmul(rank_ps[:, n:2 * n], const("ones"), flat, start=True, stop=True).then_inc(rank_done, 1)

            def clear_state():
                pe.wait_ge(c_loaded, 16)
                pe.wait_ge(set_up, 1)
                pe.matmul(state_ps, zero[:, 0:P], zero[:, :], start=True, stop=False, skip_group_check=True)\
                  .then_inc(state_zero, 1)

            pe.wait_ge(w_loaded, 16)

            def step(g, m, route):
                if route == 2:
                    if exists(g, m - 1):
                        prefix(g, m - 1)
                    if exists(g, m + 2):
                        project(g, m + 2)
                    pe.wait_ge(qT_done, GROUP * g + m if exists(g, m - 1) else CHUNKS)
                    turn_z(g - 1)
                    if exists(g, m - 1):
                        state(g, m - 1)
                    pe.wait_ge(y_used, GROUP * g + m - 2 if exists(g, m - 3) else CHUNKS)
                    logits(g - 1)
                    if exists(g, m - 2):
                        turn_o(g, m - 2)
                        pe.wait_ge(lgs_done, g)
                        put_out(g, m - 2)
                    return
                first = isinstance(g, int) and g == 0 and m == 1
                if exists(g, m + 2) and not first:
                    project(g, m + 2)
                if isinstance(g, int) and g == 0 and m == -1:
                    clear_state()
                if exists(g, m - 1):
                    prefix(g, m - 1)
                if first:
                    project(g, m + 2)
                if exists(g, m - 2):
                    turn_o(g, m - 2)
                if route == 3 and exists(g, m - 1):
                    pe.wait_ge(inter_used, GROUP * g + m - 1)
                    ranks(g - 1)
                    pe.wait_ge(rank_used, g)
                if exists(g, m - 1):
                    state(g, m - 1)
                if exists(g, m - 2):
                    if isinstance(g, int) and g == 0 and m == 2:
                        pe.wait_ge(set_up, 3)
                        pe.wait_ge(wr_loaded, 32)
                        pe.wait_ge(x_loaded, 16)
                    put_out(g, m - 2)
                if route == 3 and not exists(g, m - 1):
                    ranks(g - 1)

            groups(pe, step)
            last = GROUPS - 1
            turn_last_z()
            last_logits()
            ranks(last)

            expert = [pe.alloc_register(f"expert{b}") for b in range(4)]

            def look_up(k, b):
                pe.reg_load(expert[b % 4], tile_e[0:1, at(k)])

            def expert_of(b):
                return pe.snap(expert[b % 4], min_val=0, max_val=E - 1)

            def turn_in(k, b, rnd):
                pe.wait_ge(zin_loaded[b], 16 * (rnd + 1))
                pe.transpose(zinT_ps[b % 2][:, 0:P], zin[:, b, 0:D], const("ident")).then_inc(zinTp_done, 1)

            def gates(k, b, rnd):
                e = expert_of(b)
                hi, lo = w_hi[:, bass.ds(e, 1), :], w_lo[:, bass.ds(e, 1), :]
                hi, lo = (w.rearrange("p e h -> p (e h)") for w in (hi, lo))
                pe.wait_ge(zin_lo_done, k + 1)
                g = gate_ps[b % 2][:, :]
                pe.matmul(g, zin_hi[:, b % 2, :], hi, start=True, stop=False)
                pe.matmul(g, zin_hi[:, b % 2, :], lo, start=False, stop=False)
                pe.matmul(g, zin_lo[:, b % 2, :], hi, start=False, stop=True).then_inc(gate_done, 1)
                if not isinstance(k, int) or k + 1 < TILES:
                    look_up(k + 1, b + 1)

            def output(k, b, rnd):
                e = expert_of(b)
                pe.wait_ge(actT_done, k + 1)
                for h in range(HB):
                    mm = pe.matmul(yout_ps[b % 2][:, 0:D], actT[:, b % 2, h, :],
                                   w_l[:, bass.ds(e * (HB * D) + h * D, D)], start=(h == 0), stop=(h == HB - 1))
                mm.then_inc(yp_done, 1)

            def turn_act(k, b, rnd):
                pe.wait_ge(act_done, k + 1)
                for h in range(HB):
                    mm = pe.transpose(actT_ps[b % 2][:, h * P:(h + 1) * P], act[:, b % 2, h * P:(h + 1) * P],
                                      const("ident"))
                mm.then_inc(actTp_done, 1)

            pe.wait_ge(w_lo_done, E)
            pe.wait_ge(wl_loaded, 16)
            pe.wait_ge(table_done, 1)
            pe.wait_ge(route_done, GROUPS)
            look_up(0, 0)
            tiles(pe, (0, turn_in), (1, gates), (3, output), (2, turn_act))

            pe.wait_ge(z_saved, 16 * (GROUPS + 1))
            pe.wait_ge(yout_done, TILES)
            for g in PE_PAIRS:
                c = slice(PAIR * g, PAIR * g + PAIR)
                pe.matmul(sum_ps[g], const("ident"), zall[:, c, :].rearrange("p c d -> p (c d)"),
                          start=True, stop=False)
            for g in PE_PAIRS:
                c = slice(PAIR * g, PAIR * g + PAIR)
                pe.wait_ge(pl_loaded[g], 16)
                pe.matmul(sum_ps[g], const("ident"), pl[:, c, 0, :], start=False, stop=False)
                pe.matmul(sum_ps[g], const("ident"), pl[:, c, 1, :], start=False, stop=True).then_inc(sum_done, 1)

        @block.scalar
        def _(ac):
            def inputs(g, m):
                n = GROUP * g + m
                ac.wait_ge(qkv_done, n + 1)
                after(ac, phi_done, n - 1)
                ac.activation(eqk[:, m % 2, :], qkv_ps[:, 0:2 * D], ACT.Exp).then_inc(act_in, 1)
                ac.activation(rqk[:, m % 2, :], qkv_ps[:, 0:2 * D], ACT.Relu).then_inc(act_in, 1)
                after(ac, state_done, n - GROUP + 1)
                after(ac, kv_done, n - GROUP + 1)
                ac.activation(v1[:, m % GROUP, :].rearrange("p (h e) -> p h e", e=HE)[:, :, 0:HD],
                              qkv_ps[:, 2 * D:3 * D].rearrange("p (h d) -> p h d", d=HD),
                              ACT.Copy).then_inc(act_in, 1)

            def copy_qT(g, m):
                n = GROUP * g + m
                ac.wait_ge(qTp_done, n + 1)
                after(ac, inter_done, n - 1)
                ac.copy(qT[:, m % 2, :], qT_ps).then_inc(qT_done, 1)

            def copy_oT(g, m):
                n = GROUP * g + m
                ac.wait_ge(oTp_done, n + 1)
                after(ac, y_done, n - 1)
                ac.copy(oT[:, m % 2, :], oT_ps).then_inc(oT_done, 1)

            def copy_y(g, m, aside):
                n, s = GROUP * g + m, m % GROUP
                ac.wait_ge(y_done, n + 1)
                after(ac, negm_done, g + m // GROUP)
                ac.activation(y[:, GROUP if aside else s, :], y_ps, ACT.Identity,
                              accum_out=ysum[:, s:s + 1]).then_inc(y_used, 1)

            def spread(g, chunks=range(GROUP)):
                ac.wait_ge(negm_done, g + 2 if is_last(g) and GROUP - 1 in chunks else g + 1)
                after(ac, y_moved, g)
                for i in chunks:
                    after(ac, ssq_done, GROUP * g + i)
                    ac.activation(junk[:, 0, :], y[:, i, :], ACT.Square, bias=negm[:, i:i + 1],
                                  accum_out=ssq[:, i:i + 1]).then_inc(ssq_done, 1)

            def normalise(g, chunks=range(GROUP)):
                ac.wait_ge(shift_done, g + 1)
                ac.wait_ge(rstd_done, g + 1)
                after(ac, rows_done, GROUP * g)
                ac.wait_ge(z_saved, 16 * (g + 1))
                for i in chunks:
                    ac.activation(zs[:, i, :], y[:, i, :], ACT.Identity, bias=shift[:, i:i + 1],
                                  scale=rstd[:, i:i + 1]).then_inc(z_done, 1)

            def move_y(g):
                ac.wait_ge(z_done, GROUP * g + GROUP)
                ac.wait_ge(y_used, GROUP * g + GROUP + 1)
                ac.copy(y[:, 0, :], y[:, GROUP, :]).then_inc(y_moved, 1)

            def squares(g, chunks=range(GROUP)):
                for i in chunks:
                    ac.wait_ge(z_done, GROUP * g + i + 1)
                    after(ac, zsq_done, GROUP * g + i)
                    ac.activation(junk[:, 1, :], zs[:, i, :], ACT.Square,
                                  accum_out=zsq[:, i:i + 1]).then_inc(zsq_done, 1)

            def copy_zT(g):
                ac.wait_ge(zTp_done, g + 1)
                ac.copy(zT[:, :, :].rearrange("p c t -> p (c t)"), turn_ps[:, :]).then_inc(zT_done, 1)

            def copy_last_zT():
                for half, turned in enumerate((turn_ps, qkv_ps)):
                    chunks = slice(half * GROUP // 2, (half + 1) * GROUP // 2)
                    ac.wait_ge(zTp_done, GROUPS + half)
                    ac.copy(zT[:, chunks, :].rearrange("p c t -> p (c t)"),
                            turned[:, chunks.start * P:chunks.stop * P]).then_inc(zT_done, 1)

            def copy_logits(g):
                ac.wait_ge(lg_done, g + 1)
                ac.copy(lgs[:, :, :].rearrange("p c e -> p (c e)"), lg_ps).then_inc(lgs_done, 1)

            def fill_rows(g):
                if is_last(g):
                    ac.wait_ge(v_z_done, GROUP // 2)
                wait_for_rows(ac, g)
                for i in range(GROUP):
                    ac.activation(rows_of(g)[:, i, :, 0:D], zs[:, i, :].unsqueeze(1).to_broadcast([P, K, D]),
                                  ACT.Copy).then_inc(rows_done, 1)

            def exp_logits(g):
                ac.wait_ge(dlog_done, g + 1)
                ac.activation(R["elog"][:, :, :], R["dlog"][:, :, :], ACT.Exp).then_inc(elog_done, 1)

            def split_weights(i):
                ac.wait_ge(wg_loaded[i], 16)
                for e in range(i * E // GROUP, (i + 1) * E // GROUP):
                    ac.copy(w_hi[:, e, :], w_g[:, e, :]).then_inc(w_hi_done, 1)

            ac.preload_act_table_set("exp_and_others")
            ac.wait_ge(pool_set_up, 1)

            def step(g, m, route):
                if route == 1:
                    if exists(g, m - 1):
                        copy_qT(g, m - 1)
                    if exists(g, m - 2):
                        copy_oT(g, m - 2)
                    normalise(g - 1)
                    if exists(g, m - 3):
                        move_y(g - 1)
                    if exists(g, m + 2):
                        inputs(g, m + 2)
                elif route == 2:
                    if exists(g, m - 1):
                        copy_qT(g, m - 1)
                    squares(g - 1)
                    copy_zT(g - 1)
                    if exists(g, m + 2):
                        inputs(g, m + 2)
                    copy_logits(g - 1)
                    if exists(g, m - 2):
                        copy_oT(g, m - 2)
                else:
                    if exists(g, m + 2):
                        inputs(g, m + 2)
                    if exists(g, m - 1):
                        copy_qT(g, m - 1)
                    if exists(g, m - 2):
                        copy_oT(g, m - 2)
                if route == 0:
                    spread(g - 1)
                if route == 3 and is_last(g):
                    spread(g, (2,))
                if exists(g, m - 2):
                    copy_y(g, m - 2, route == 0)
                if route == 2:
                    if is_last(g):
                        fill_rows(g - 1)
                    exp_logits(g - 1)
                    if is_last(g):
                        spread(g, (0, 1))
                if route == 3:
                    if is_last(g):
                        spread(g, (3,))
                    else:
                        fill_rows(g - 1)
                if isinstance(g, int) and g == 0 and m >= 2:
                    split_weights(m - 2)

            groups(ac, step)
            last = GROUPS - 1
            ahead = range(GROUP // 2)
            normalise(last, ahead)
            squares(last, ahead)
            copy_last_zT()
            copy_logits(last)
            exp_logits(last)
            ac.preload_act_table_set("gelu_apprx_tanh_and_others")
            fill_rows(last)

            def split_zin(k, b, rnd):
                ac.wait_ge(zinTp_done, k + 1)
                ac.copy(zin_hi[:, b % 2, :], zinT_ps[b % 2][:, 0:P]).then_inc(zin_hi_done, 1)

            def gelu_gate(k, b, rnd):
                ac.wait_ge(gate_done, k + 1)
                ac.activation(gelu[:, b % 2, :], gate_ps[b % 2][:, 0:HID], ACT.Gelu_apprx_tanh).then_inc(gelu_done, 1)

            def copy_actT(k, b, rnd):
                ac.wait_ge(actTp_done, k + 1)
                ac.copy(actT[:, b % 2, :, :].rearrange("p h t -> p (h t)"), actT_ps[b % 2][:, 0:HID])\
                  .then_inc(actT_done, 1)

            tiles(ac, (0, split_zin), (1, gelu_gate), (2, copy_actT))

            for g in range(V_PAIR):
                ac.wait_ge(fshift_done, g + 1)
                ac.wait_ge(frs_done, g + 1)
                for j in range(PAIR):
                    i = PAIR * g + j
                    ac.activation(res[:, i, :], total_of(g)[:, j, :], ACT.Identity, bias=fshift[:, i:i + 1],
                                  scale=frs[:, i:i + 1]).then_inc(res_done, 1)

        @block.vector
        def _(ve):
            st = Steps(ve, dve_steps)
            ve.memset(zero[:, :], 0.0).then_inc(set_up, 1)
            ve.wait_ge(c_loaded, 16)
            ve.tensor_copy(tok[:, :], const("tok")).then_inc(set_up, 1)
            ve.wait_ge(wr_loaded, 32)
            ve.wait_ge(scattered, 16)
            ve.wait_ge(z_saved, 16)
            ve.tensor_scalar(w_r[:, :], w_r0[:, :], w_rs[:, 0:1], None, ALU.mult).then_inc(set_up, 1)
            st.chain(ve.tensor_copy(base[:, 0, :], const("ebase")))
            lead = st.n

            def heads(t, n=H):
                return t.rearrange("p (h e) -> p h e", e=HE)

            def features(g, m):
                n, s = GROUP * g + m, m % GROUP
                ve.wait_ge(act_in, 3 * (n + 1))
                after(ve, state_done, n - GROUP + 1)
                after(ve, kv_done, n - GROUP + 1)
                ve.scalar_tensor_tensor(out=qk[:, s, :], in0=eqk[:, m % 2, :], scalar=1.0, in1=rqk[:, m % 2, :],
                                        op0=ALU.min, op1=ALU.add).then_inc(phi_done, 1)

            def mask_state(g, m):
                n = GROUP * g + m
                if isinstance(g, int) and n < 1:
                    ve.wait_ge(state_zero, 1)
                else:
                    ve.wait_ge(state_done, n)
                after(ve, inter_done, n - 1)
                ve.tensor_tensor(state_m[:, m % 2, :], state_ps, const("block"), ALU.mult).then_inc(state_used, 1)

            def attend(g, m, between):
                n, s = GROUP * g + m, m % GROUP
                q = qk[:, s, 0:D].rearrange("p (h d) -> p h d", d=HD)
                for b, (h0, h1) in enumerate(HEADS):
                    ve.wait_ge(pre_done, 3 * n + b + 1)
                    if b == 0:
                        after(ve, summed, n)
                    nh = h1 - h0
                    cols = nh * HE * HD
                    ve.tensor_tensor(
                        prod[:, h0 * HE * HD:h1 * HE * HD].rearrange("p (h e d) -> p h e d", e=HE, d=HD),
                        pre_ps[b][:, 0:cols].rearrange("p (h e d) -> p h e d", e=HE, d=HD),
                        q[:, h0:h1, :].unsqueeze(2).to_broadcast([P, nh, HE, HD]), ALU.mult).then_inc(pre_used, 1)
                    between(b)
                ve.wait_ge(pre_used, 3 * (n + 1))
                after(ve, inter_used, n)
                ve.tensor_reduce(num[:, :], prod[:, :].rearrange("p (c d) -> p c d", d=HD), AX.X,
                                 ALU.add).then_inc(summed, 1)
                between(3)
                if exists(g, m + 1):
                    mask_state(g, m + 1)
                between(4)
                ve.wait_ge(inter_done, n + 1)
                ve.wait_ge(summed, n + 1)
                after(ve, o_done, n)
                ve.tensor_tensor(num2[:, :], inter_ps, num[:, :], ALU.add).then_inc(inter_used, 1)
                if exists(g, m + 3):
                    features(g, m + 3)
                between(5)
                ve.wait_ge(inter_used, n + 1)
                ve.tensor_scalar(den[:, :], heads(num2[:, :])[:, :, HD], DEN_MIN, None, ALU.max).then_inc(den_done, 1)
                between(6)
                ve.wait_ge(den_done, n + 1)
                ve.reciprocal(rden[:, :], den[:, :]).then_inc(rden_done, 1)
                between(7)
                ve.wait_ge(rden_done, n + 1)
                after(ve, oTp_done, n - 1)
                ve.tensor_tensor(o[:, m % 2, :].rearrange("p (h d) -> p h d", d=HD), heads(num2[:, :])[:, :, 0:HD],
                                 rden[:, :].unsqueeze(2).to_broadcast([P, H, HD]), ALU.mult).then_inc(o_done, 1)
                between(8)

            def by_token(t):
                return t.unsqueeze(2).to_broadcast([P, GROUP, E])

            def by_rank(t):
                return t.unsqueeze(1).to_broadcast([P, K, GROUP, E])

            def tt(out, a, b, op, last=0):
                st.ready(last)
                st.did(ve.tensor_tensor(out, a, b, op))

            def ts(out, a, s1, s2, op0, op1=None, last=0):
                st.ready(last)
                st.did(ve.tensor_scalar(out, a, s1, s2, op0) if op1 is None else
                       ve.tensor_scalar(out, a, s1, s2, op0, op1))

            def reduce(out, a, op, last=0):
                st.ready(last)
                st.did(ve.tensor_reduce(out, a, AX.X, op))

            def inverse(out, a, last=0):
                st.ready(last)
                st.did(ve.reciprocal(out, a))

            def copy(out, a, last=0):
                st.ready(last)
                st.did(ve.tensor_copy(out, a))

            desc = const("desc").rearrange("p (c e) -> p c e", e=E)
            A = {n: t[:, :, :] for n, t in R.items()} | {n: t[:, :] for n, t in R1.items()}
            rank_of, tot_of = rank[:, 0], rank[:, 1]

            def mean(g, a, b):
                ve.wait_ge(y_used, GROUP * g + b)
                ve.tensor_scalar(negm[:, a:b], ysum[:, a:b], -1.0 / D, None, ALU.mult).then_inc(negm_done, 1)

            def mean_and_variance(g, i):
                if i == 1:
                    mean(g, 0, GROUP)
                if i == 4:
                    ve.wait_ge(ssq_done, GROUP * g + GROUP)
                    ve.tensor_scalar(vare[:, :], ssq[:, :], 1.0 / D, LN_EPS, ALU.mult, ALU.add)\
                      .then_inc(vare_done, 1)
                if i == 8:
                    ve.wait_ge(rstd_done, g + 1)
                    ve.wait_ge(negm_done, g + 2 if is_last(g) else g + 1)
                    ve.tensor_tensor(shift[:, :], negm[:, :], rstd[:, :], ALU.mult).then_inc(shift_done, 1)

            def choose(g, i):
                if i == 1:
                    if is_last(g):
                        ve.wait_ge(zsq_done, GROUP * g + GROUP // 2)
                        ve.wait_ge(v_zsq_done, GROUP // 2)
                    else:
                        ve.wait_ge(zsq_done, GROUP * g + GROUP)
                    ve.tensor_scalar(zsqe[:, :], zsq[:, :], D * RMS_EPS, None, ALU.add).then_inc(zsqe_done, 1)
                if i == 3:
                    ve.wait_ge(lgs_done, g + 1)
                    ve.wait_ge(rrms_done, g + 1)
                    tt(A["logit"], lgs[:, :, :], by_token(rrms[:, :]), ALU.mult)
                if i == 4:
                    reduce(A["m1"], A["logit"], ALU.max)
                    tt(A["eq1"], A["logit"], by_token(A["m1"]), ALU.is_equal)
                if i == 5:
                    tt(A["key1"], A["eq1"], desc, ALU.mult)
                    reduce(A["k1"], A["key1"], ALU.max)
                if i == 6:
                    tt(A["ind1"], desc, by_token(A["k1"]), ALU.is_equal)
                    ve.tensor_tensor(A["dlog"], A["logit"], by_token(A["m1"]), ALU.subtract).then_inc(dlog_done, 1)
                    st.ready()
                    st.did(ve.scalar_tensor_tensor(out=A["rest"], in0=A["ind1"], scalar=BELOW, in1=A["logit"],
                                                   op0=ALU.mult, op1=ALU.add))
                if i == 7:
                    reduce(A["m2"], A["rest"], ALU.max)
                    tt(A["eq2"], A["rest"], by_token(A["m2"]), ALU.is_equal)
                if i == 8:
                    tt(A["key2"], A["eq2"], desc, ALU.mult)
                    reduce(A["k2"], A["key2"], ALU.max)
                    tt(A["ind2"], desc, by_token(A["k2"]), ALU.is_equal)
                    st.ready()
                    ve.tensor_tensor(A["ind"], A["ind1"], A["ind2"], ALU.add).then_inc(ind_done, 1)

            def weigh_and_place(g, i):
                if i == 0:
                    ve.wait_ge(elog_done, g + 1)
                    reduce(A["esum"], A["elog"], ALU.add)
                    inverse(A["einv"], A["esum"])
                if i == 1:
                    ve.wait_ge(ind_done, g + 1)
                    tt(A["prob"], A["elog"], by_token(A["einv"]), ALU.mult)
                    tt(A["gw"], A["prob"], A["ind"], ALU.mult)
                if i == 2:
                    reduce(A["ren"], A["gw"], ALU.add)
                    ve.wait_ge(rank_done, 2 * g + 2)
                    ve.tensor_copy(rank[:, :, :, :].rearrange("p k c e -> p (k c e)"), rank_ps)\
                      .then_inc(rank_used, 1)
                if i == 3:
                    st.ready()
                    st.did(ve.scalar_tensor_tensor(out=A["reng"], in0=A["ren"], scalar=0.0, in1=A["ren"],
                                                   op0=ALU.is_le, op1=ALU.add))
                    ve.wait_ge(rank_used, g + 1)
                    tt(base[:, 1, :], tot_of[:, 0, :], base[:, 0, :], ALU.add, last=1)
                if i == 4:
                    inverse(A["renr"], A["reng"], last=1)
                    tt(base[:, 2, :], tot_of[:, 1, :], base[:, 1, :], ALU.add, last=1)
                if i == 5:
                    tt(A["comb"], A["gw"], by_token(A["renr"]), ALU.mult, last=1)
                    tt(base[:, 3, :], tot_of[:, 2, :], base[:, 2, :], ALU.add, last=1)
                if i == 6:
                    tt(A["combs"], A["comb"], pes_b[:, :].unsqueeze(1).to_broadcast([P, GROUP, E]), ALU.mult, last=1)
                    tt(base[:, 4, :], tot_of[:, 3, :], base[:, 3, :], ALU.add, last=1)
                if i == 7:
                    tt(comb12[:, :, :, :], by_rank(A["combs"]), ind12[:, :, :, :], ALU.mult, last=1)
                    tt(A["pos"], rank_of, base[:, 0:GROUP, :], ALU.add, last=1)
                if i == 8:
                    to = rows_of(g)
                    wait_for_rows(ve, g)
                    reduce(to[:, :, :, D].rearrange("p c r -> p r c"), comb12[:, :, :, :], ALU.add, last=1)
                    tt(pos12[:, :, :, :], by_rank(A["pos"]), ind12[:, :, :, :], ALU.mult, last=1)
                    copy(to[:, :, :, D + 1].bitcast(I32).rearrange("p c r -> p r c"),
                         tok[:, :].rearrange("p (r c) -> p r c", c=GROUP), last=1)
                    reduce(slot_f[:, :].rearrange("p (r c) -> p r c", c=GROUP), pos12[:, :, :, :], ALU.add, last=1)
                    ts(tok[:, :], tok[:, :], float(K * GROUP * P), None, ALU.add, last=1)
                    copy(base[:, 0, :], base[:, GROUP, :], last=1)
                    st.ready(2)
                    ve.tensor_copy(slot_of(g)[:, :], slot_f[:, :]).then_inc(route_done, 1)

            behind = range(GROUP // 2, GROUP)

            def normalise_behind():
                ve.wait_ge(shift_done, GROUPS)
                ve.wait_ge(rows_done, CHUNKS - GROUP)
                ve.wait_ge(z_saved, 16 * GROUPS)
                for i in behind:
                    ve.tensor_scalar(zs[:, i, :], y[:, i, :], rstd[:, i:i + 1], shift[:, i:i + 1], ALU.mult,
                                     ALU.add).then_inc(v_z_done, 1)

            def squares_behind():
                for i in behind:
                    ve.wait_ge(v_z_done, i - GROUP // 2 + 1)
                    if i > GROUP // 2:
                        ve.wait_ge(v_zsq_done, i - GROUP // 2)
                    ve.scalar_tensor_tensor(out=junk[:, 0, :], in0=zs[:, i, :], scalar=1.0, in1=zs[:, i, :],
                                            op0=ALU.mult, op1=ALU.mult,
                                            accum_out=zsq[:, i:i + 1]).then_inc(v_zsq_done, 1)

            parts = (mean_and_variance, lambda g, i: None, choose, weigh_and_place)

            def step(g, m, route):
                def between(i):
                    if route == 2 and i == 5 and is_last(g):
                        mean(g, 0, GROUP - 1)
                    if route is not None:
                        parts[route](g - 1, i)
                if route == 0 and (not isinstance(g, int) or g > 1):
                    ve.wait_ge(route_done, g - 1)
                if exists(g, m - 1):
                    attend(g, m - 1, between)
                else:
                    if exists(g, m + 2):
                        features(g, m + 2)
                    if isinstance(g, int) and g == 0 and m == 0:
                        mask_state(0, 0)
                    for i in range(9):
                        if route == 3 and i == 2:
                            mean(g, GROUP - 1, GROUP)
                        if route == 3 and i == 5:
                            mean_and_variance(g, 4)
                        if route == 3 and i == 8:
                            mean_and_variance(g, 8)
                            normalise_behind()
                        between(i)

            ROUTE_STEPS = 12 + 21
            groups(ve, step, lambda g: st.start(lead + ROUTE_STEPS * (g - 1)))
            assert st.n == ROUTE_STEPS, st.n
            last = GROUPS - 1
            st.start(lead + ROUTE_STEPS * last)
            ve.wait_ge(route_done, last)
            squares_behind()
            for part in parts[1:]:
                for i in range(9):
                    part(last, i)
            st.ready()
            assert st.n == ROUTE_STEPS, st.n

            ve.tensor_copy(cnt_i[:, :], base[:, 0, :]).then_inc(cnt_done, 1)
            st.chain(ve.scalar_tensor_tensor(out=nt_f[:, :], in0=base[:, 0, :], scalar=float(P - 1),
                                             in1=const("ebase"), op0=ALU.add, op1=ALU.subtract))
            st.chain(ve.tensor_copy(nt_i[:, :], nt_f[:, :]))
            st.chain(ve.tensor_scalar(nt_s[:, :], nt_i[:, :], P.bit_length() - 1, None, ALU.arith_shift_right))
            st.chain(ve.tensor_copy(ntile[:, :], nt_s[:, :]))
            cum = ntile
            for by, nxt in ((1, cumA), (2, cumB), (4, cumC)):
                st.did(ve.tensor_copy(nxt[:, 0:by], cum[:, 0:by]))
                st.chain(ve.tensor_tensor(nxt[:, by:E], cum[:, by:E], cum[:, 0:E - by], ALU.add))
                cum = nxt
            st.chain(ve.tensor_scalar(skip[:, :], ntile[:, :], float(-P), float(REGION), ALU.mult, ALU.add))
            a, b = CONST["tile"]
            num_t = C[0:1, a:b]
            tt(past[:, :, :], cum[0:1, :].unsqueeze(1).to_broadcast([1, TILES, E]),
               num_t.unsqueeze(2).to_broadcast([1, TILES, E]), ALU.is_le)
            st.ready()
            tt(pskip[:, :, :], past[:, :, :], skip[0:1, :].unsqueeze(1).to_broadcast([1, TILES, E]), ALU.mult)
            st.ready()
            st.chain(ve.tensor_reduce(te_f[:, :], past[:, :, :], AX.X, ALU.add))
            st.chain(ve.tensor_reduce(tr_f[:, :], pskip[:, :, :], AX.X, ALU.add))
            st.chain(ve.tensor_scalar(te_g[:, :], te_f[:, :], float(E - 1), None, ALU.min))
            st.chain(ve.tensor_copy(tile_e[:, :], te_g[:, :]))
            st.chain(ve.scalar_tensor_tensor(out=tr_g[:, :], in0=num_t, scalar=float(P), in1=tr_f[:, :],
                                             op0=ALU.mult, op1=ALU.add))
            ve.tensor_copy(tile_r[:, :], tr_g[:, :]).then_inc(table_done, 1)
            ve.wait_ge(table_done, 1)

            ve.wait_ge(w_hi_done, E)
            for e in range(E):
                ve.tensor_tensor(w_lo[:, e, :], w_g[:, e, :], w_hi[:, e, :].bitcast(F32),
                                 ALU.subtract).then_inc(w_lo_done, 1)

            def rest_zin(k, b, rnd):
                ve.wait_ge(zin_hi_done, k + 1)
                ve.tensor_tensor(zin_lo[:, b % 2, :], zinT_ps[b % 2][:, 0:P], zin_hi[:, b % 2, :].bitcast(F32),
                                 ALU.subtract).then_inc(zin_lo_done, 1)

            def activate(k, b, rnd):
                ve.wait_ge(gelu_done, k + 1)
                ve.scalar_tensor_tensor(out=act[:, b % 2, :], in0=gelu[:, b % 2, :], scalar=zin[:, b, D:D + 1],
                                        in1=gate_ps[b % 2][:, HID:2 * HID], op0=ALU.mult, op1=ALU.mult)\
                  .then_inc(act_done, 1)

            def take(k, b, rnd):
                ve.wait_ge(yp_done, k + 1)
                ve.tensor_copy(yout[:, b, :], yout_ps[b % 2][:, 0:D]).then_inc(yout_done, 1)

            tiles(ve, (0, rest_zin), (3, take), (1, activate))

            ve.wait_ge(z_saved, 16 * (GROUPS + 1))

            def total(g):
                c = slice(PAIR * g, PAIR * g + PAIR)
                if g in POOL_PAIRS:
                    ve.wait_ge(s1_done, POOL_PAIRS.index(g) + 1)
                else:
                    ve.wait_ge(pl_loaded[g], 16)
                    ve.tensor_tensor(s1[:, c, :], pl[:, c, 0, :], pl[:, c, 1, :], ALU.add).then_inc(s1v_done, 1)
                    ve.wait_ge(s1v_done, sum(h not in PE_PAIRS + POOL_PAIRS for h in range(g + 1)))
                ve.tensor_tensor(s2[:, c, :], s1[:, c, :], zall[:, c, :], ALU.add).then_inc(s2_done, 1)

            def statistics(g):
                if g in PE_PAIRS:
                    ve.wait_ge(sum_done, PE_PAIRS.index(g) + 1)
                else:
                    ve.wait_ge(s2_done, sum(h not in PE_PAIRS for h in range(g + 1)))
                for j in range(PAIR):
                    ve.bn_stats(fstat[:, PAIR * g + j, :], total_of(g)[:, j, :]).then_inc(fstat_done, 1)

            def aggregate(g):
                ve.wait_ge(fstat_done, PAIR * (g + 1))
                for i in range(PAIR * g, PAIR * g + PAIR):
                    ve.bn_aggr(fmv[:, i, :], fstat[:, i, :]).then_inc(fmv_done, 1)

            def variances(g):
                c = slice(PAIR * g, PAIR * g + PAIR)
                ve.wait_ge(fmv_done, PAIR * (g + 1))
                ve.tensor_scalar(fvar[:, c], fmv[:, c, 1], LN_EPS, None, ALU.add).then_inc(fvar_done, 1)

            def shifts(g):
                c = slice(PAIR * g, PAIR * g + PAIR)
                ve.wait_ge(frs_done, g + 1)
                ve.scalar_tensor_tensor(out=fshift[:, c], in0=fmv[:, c, 0], scalar=-1.0, in1=frs[:, c],
                                        op0=ALU.mult, op1=ALU.mult).then_inc(fshift_done, 1)

            for g in range(PAIRS + 2):
                if g < PAIRS and g not in PE_PAIRS:
                    total(g)
                if 1 <= g <= PAIRS:
                    aggregate(g - 1)
                if g < PAIRS:
                    statistics(g)
                if 1 <= g <= PAIRS:
                    variances(g - 1)
                if g >= 2:
                    shifts(g - 2)
            ve.wait_ge(fshift_done, PAIRS)
            for j in range(PAIR):
                i = PAIR * V_PAIR + j
                ve.tensor_scalar(res[:, i, :], total_of(V_PAIR)[:, j, :], frs[:, i:i + 1], fshift[:, i:i + 1],
                                 ALU.mult, ALU.add).then_inc(res_v_done, 1)


def constants():
    import numpy as np

    c = np.zeros((P, NCONST), np.float32)
    i = np.arange(P)

    def put(name, v):
        a, b = CONST[name]
        c[:, a:b] = v

    put("tri", i[:, None] <= i[None, :])
    put("stri", i[:, None] < i[None, :])
    put("ident", np.eye(P))
    put("ones", 1.0)
    put("block", (i[:, None] // HD) == (np.arange(H * HE)[None, :] // HE))
    put("desc", np.tile(E - np.arange(E), GROUP)[None, :])
    put("tok", K * i[:, None] + (np.arange(K)[:, None] + K * P * np.arange(GROUP)[None, :]).reshape(1, -1))
    put("ebase", (np.arange(E) * REGION)[None, :])
    put("tile", np.arange(TILES)[None, :])
    put("half", -0.5)
    put("pad", K * T + i[:, None] + P * np.arange(PADS)[None, :])
    return c


def kernel(**inputs):
    import numpy as np
    import concourse.bacc as bacc
    from concourse.bass_utils import run_bass_kernel_spmd

    a = {k: np.asarray(v) for k, v in inputs.items()}
    x = a["L0_attn_x"].reshape(T, D)
    wqkv = np.concatenate([a["L0_attn_Wq"].T, a["L0_attn_Wk"].T, a["L0_attn_Wv"].T], axis=1)
    arrays = {
        "xT": x.T,
        "x": x,
        "wqkv": wqkv,
        "wo": a["L0_attn_Wo"].T,
        "rw": a["L0_ffn_router_w"],
        "rscale": a["L0_ffn_router_scale"].reshape(D, 1),
        "pes": np.broadcast_to(a["L0_ffn_per_expert_scale"].reshape(1, E), (P, E)),
        "gate_w": a["L0_ffn_gating_w"].transpose(3, 0, 1, 2).reshape(D, E * 2 * HID),
        "lin_w": a["L0_ffn_linear_w"].reshape(E, HB, P, D).transpose(2, 0, 1, 3).reshape(P, E * HB * D),
        "consts": constants(),
    }
    arrays = {k: np.ascontiguousarray(v) for k, v in arrays.items()}
    nc = bacc.Bacc("TRN2", target_bir_lowering=False, num_devices=1)
    args = [nc.dram_tensor("in_" + k, v.shape, F32, kind="ExternalInput").ap() for k, v in arrays.items()]
    out = nc.dram_tensor("out_0", (T, D), F32, kind="ExternalOutput").ap()
    build(nc, *args, out)
    r = run_bass_kernel_spmd(nc, [{"in_" + k: v for k, v in arrays.items()}], core_ids=[0])
    return r.results[0]["out_0"].reshape(1, T, D)
```
